# Optimizing a Trainium2 kernel written in Bass

```python
import numpy as np
import jax
import jax.numpy as jnp

def _softmax(x, axis=-1):
    return jax.nn.softmax(x, axis=axis)

def _gelu(x):
    return jax.nn.gelu(x, approximate=True)

def _silu(x):
    return jax.nn.silu(x)

def _sigmoid(x):
    return jax.nn.sigmoid(x)

def _layernorm(x, axis=-1, eps=1e-05):
    m = jnp.mean(x, axis=axis, keepdims=True)
    v = jnp.var(x, axis=axis, keepdims=True)
    return (x - m) / jnp.sqrt(v + eps)

def _scatter_add(tgt, idx, src, axis=0):
    return tgt.at[idx].add(src)

def _segment_sum(src, seg, n):
    return jax.ops.segment_sum(src, seg, n)
kernel_name = 'mk_conv_preact_d1_conv_nchw256_r2_0a0aba'

def setup_inputs(seed: int=0):
    np.random.seed(seed)
    _w = jnp.asarray

    def _rec_inputs():
        import jax
        import jax.numpy as jnp
        _gk = jax.random.key(seed)
        x = -9.26e-05 + 0.9999 * jax.random.normal(jax.random.fold_in(_gk, 1), (4, 128, 96, 96), jnp.float32)
        return x
    x = _rec_inputs()

    def _L0_conv_setup():
        import jax, jax.numpy as jnp
        from jax import lax
        import numpy as np
        WS = 4
        DIM = 8
        HEADS = 32
        TOT = 128
        CIN = 128
        COUT = 128
        NS = 1
        BN_EPS = 1e-05

        def _avg_pool5(x):
            s = lax.reduce_window(x, 0.0, lax.add, (1, 1, 5, 5), (1, 1, 1, 1), [(0, 0), (0, 0), (2, 2), (2, 2)])
            return s / 25.0
        key = jax.random.key(seed)
        k0, k1, k2 = jax.random.split(key, 3)
        B, H, W = (4, 96, 96)
        x = jax.random.normal(k0, (B, CIN, H, W), jnp.float32)
        qkv_w = jax.random.normal(k1, (3 * TOT, CIN), jnp.float32) * 0.02
        proj_w = jax.random.normal(k2, (COUT, TOT * (1 + NS)), jnp.float32) * 0.02
        bn_gamma = jnp.ones((COUT,), jnp.float32)
        bn_beta = jnp.zeros((COUT,), jnp.float32)
        bn_mean = jnp.zeros((COUT,), jnp.float32)
        bn_var = jnp.ones((COUT,), jnp.float32)
        return {'x': x, 'qkv_w': qkv_w, 'proj_w': proj_w, 'bn_gamma': bn_gamma, 'bn_beta': bn_beta, 'bn_mean': bn_mean, 'bn_var': bn_var}
    _L0_conv_all = _L0_conv_setup()
    _L0_conv_in = {k: v for k, v in _L0_conv_all.items() if k in ('qkv_w', 'proj_w', 'bn_gamma', 'bn_beta', 'bn_mean', 'bn_var')}
    del _L0_conv_all
    return {'x': x, 'L0_conv_qkv_w': _L0_conv_in['qkv_w'], 'L0_conv_proj_w': _L0_conv_in['proj_w'], 'L0_conv_bn_gamma': _L0_conv_in['bn_gamma'], 'L0_conv_bn_beta': _L0_conv_in['bn_beta'], 'L0_conv_bn_mean': _L0_conv_in['bn_mean'], 'L0_conv_bn_var': _L0_conv_in['bn_var']}

def reference(x, L0_conv_qkv_w, L0_conv_proj_w, L0_conv_bn_gamma, L0_conv_bn_beta, L0_conv_bn_mean, L0_conv_bn_var):
    import jax
    import jax.numpy as jnp

    def _L0_conv_ref(x, qkv_w, proj_w, bn_gamma, bn_beta, bn_mean, bn_var):
        import jax, jax.numpy as jnp
        from jax import lax
        import numpy as np
        WS = 4
        DIM = 8
        HEADS = 32
        TOT = 128
        CIN = 128
        COUT = 128
        NS = 1
        BN_EPS = 1e-05

        def _avg_pool5(x):
            s = lax.reduce_window(x, 0.0, lax.add, (1, 1, 5, 5), (1, 1, 1, 1), [(0, 0), (0, 0), (2, 2), (2, 2)])
            return s / 25.0
        B, C, H, W = x.shape
        ws = WS
        Hn, Wn = (H // ws, W // ws)
        xw = x.reshape(B, C, Hn, ws, Wn, ws).transpose(0, 2, 4, 1, 3, 5)
        xw = xw.reshape(-1, C, ws, ws)
        N = xw.shape[0]
        qkv = jnp.einsum('nchw,oc->nohw', xw, qkv_w)
        pooled = _avg_pool5(qkv)
        msq = jnp.concatenate([qkv, pooled], axis=1)
        msq = msq.reshape(N, -1, 3 * DIM, ws * ws).transpose(0, 1, 3, 2)
        q = jax.nn.relu(msq[..., :DIM])
        k = jax.nn.relu(msq[..., DIM:2 * DIM])
        v = msq[..., 2 * DIM:]
        v = jnp.pad(v, ((0, 0), (0, 0), (0, 0), (0, 1)), constant_values=1.0)
        kv = jnp.einsum('ngld,nglm->ngdm', k, v)
        out = jnp.einsum('ngld,ngdm->nglm', q, kv)
        out = out[..., :-1] / (out[..., -1:] + 1e-15)
        out = out.transpose(0, 1, 3, 2).reshape(N, -1, ws, ws)
        Cw = out.shape[1]
        out = out.reshape(B, Hn, Wn, Cw, ws, ws).transpose(0, 3, 1, 4, 2, 5)
        out = out.reshape(B, Cw, H, W)
        y = jnp.einsum('nchw,oc->nohw', out, proj_w)
        inv = bn_gamma / jnp.sqrt(bn_var + BN_EPS)
        y = y * inv[None, :, None, None] + (bn_beta - bn_mean * inv)[None, :, None, None]
        return y

    def _gn(v, G=32, eps=1e-05):
        B_, C_, H_, W_ = v.shape
        g = v.reshape(B_, G, C_ // G, H_, W_)
        m = jnp.mean(g, axis=(2, 3, 4), keepdims=True)
        s = jnp.var(g, axis=(2, 3, 4), keepdims=True)
        return ((g - m) / jnp.sqrt(s + eps)).reshape(v.shape)

    def _ln_c(v, eps=1e-06):
        m = jnp.mean(v, axis=1, keepdims=True)
        s = jnp.var(v, axis=1, keepdims=True)
        return (v - m) / jnp.sqrt(s + eps)

    def _ln_t(v, eps=1e-05):
        m = jnp.mean(v, axis=-1, keepdims=True)
        s = jnp.var(v, axis=-1, keepdims=True)
        return (v - m) / jnp.sqrt(s + eps)

    def _to_tokens(v):
        B_, C_, H_, W_ = v.shape
        return v.reshape(B_, C_, H_ * W_).transpose(0, 2, 1)

    def _from_tokens(t, like):
        B_, C_, H_, W_ = like.shape
        return t.transpose(0, 2, 1).reshape(B_, C_, H_, W_)
    x = x + _L0_conv_ref(_gn(x), L0_conv_qkv_w, L0_conv_proj_w, L0_conv_bn_gamma, L0_conv_bn_beta, L0_conv_bn_mean, L0_conv_bn_var)
    return x

_drawn_inputs = setup_inputs


def setup_inputs(seed=0):
    import zlib

    import numpy as np

    out = dict(_drawn_inputs(seed))
    spreads = {'L0_conv_bn_gamma': (1.0, 0.6),
     'L0_conv_bn_beta': (0.0, 0.1),
     'L0_conv_bn_mean': (0.0, 0.1),
     'L0_conv_bn_var': (1.0, 0.6)}
    factors = {'L0_conv_qkv_w': 2.933, 'L0_conv_proj_w': 2.944}
    for name, (base, spread) in spreads.items():
        noise = np.random.default_rng([zlib.crc32(name.encode()), seed]).standard_normal(out[name].shape)
        drawn = base * np.exp(spread * noise) if base else spread * noise
        out[name] = jnp.asarray(drawn.astype(out[name].dtype))
    for name, factor in factors.items():
        out[name] = (out[name] * factor).astype(out[name].dtype)
    return out
```

```python
from contextlib import ExitStack

import numpy as np

import concourse.bass as bass
from concourse import mybir

F32 = mybir.dt.float32
ALU = mybir.AluOpType
ACT = mybir.ActivationFunctionType

P = 128
Q4 = 32
WS = 4
D = 8
GROUPS = 32
GN_EPS, BN_EPS, DEN_EPS = 1e-5, 1e-5, 1e-15

PX = WS * WS
PXP = 9
NP = WS - 1
WF = Q4 // PX
WP = Q4 // PXP
VC = Q4 + 1
KC = Q4 + 4

C_IDENT, C_GROUP = 0, P
C_HEAD = 2 * P
C_QUAD = C_HEAD + KC
C_QUADP = C_QUAD + 4
C_WF = C_QUADP + 4
C_WP = C_WF + WF
C_WPM = C_WP + WP
C_WPV = C_WPM + WP
N_CONST = C_WPV + WP


def constants():
    c = np.zeros((P, N_CONST), np.float32)
    p = np.arange(P)
    c[:, C_IDENT:C_IDENT + P] = np.eye(P)
    per = P // GROUPS
    c[:, C_GROUP:C_GROUP + P] = (p[:, None] // per == p[None] // per) / per
    head = p % Q4 // D
    c[:, C_HEAD:C_HEAD + Q4] = head[:, None] == np.arange(Q4)[None] // D
    c[:, C_HEAD + Q4:C_HEAD + KC] = head[:, None] == np.arange(4)[None]
    quad = p[:, None] // Q4 == np.arange(4)[None]
    c[:, C_QUAD:C_QUAD + 4] = quad
    c[:, C_QUADP:C_QUADP + 4] = quad / 25.0
    c[:, C_WF:C_WF + WF] = (p % Q4 // PX)[:, None] == np.arange(WF)[None]
    own = (p % Q4 // PXP)[:, None] == np.arange(WP)[None]
    side = np.array([1, 2, 1])
    times = (side[:, None] * side[None]).ravel()[p % Q4 % PXP][:, None]
    c[:, C_WP:C_WP + WP] = own
    c[:, C_WPM:C_WPM + WP] = own * times
    c[:, C_WPV:C_WPV + WP] = own * times / 25.0
    return c


def build(nc, x, wq, wkv, proj, bn, consts, out):
    B, C, H, W = x.shape
    assert C == P
    HW = H * W
    SPB = H // WS
    NS = B * SPB
    SP = WS * W
    NW = W // WS
    TF = SP // P
    TP = NW // (4 * WP)
    assert TF * P == SP and TP * 4 * WP == NW
    HALF = NW // 2
    assert HALF * KC <= 512
    TV = TF + TP
    STAT = 512
    CHUNKS = HW // STAT
    LOADS = 3
    assert CHUNKS % LOADS == 0

    x_v = x.rearrange("b c h w -> c b (h w)")
    out_v = out.rearrange("b c h w -> c b (h w)")

    with ExitStack() as ctx:
        def sb(name, shape):
            return ctx.enter_context(nc.sbuf_tensor(name, [P, *shape], F32))

        def sem(name):
            return ctx.enter_context(nc.semaphore(name))

        x_all = sb("x_all", [NS * SP])
        cst = sb("cst", [N_CONST])
        wq_sb = sb("wq_sb", [P])
        wkv_sb = sb("wkv_sb", [2 * P])
        proj_sb = sb("proj_sb", [2 * P])
        projT = sb("projT", [2 * P])
        bn_sb = sb("bn_sb", [4])
        bn_inv = sb("bn_inv", [1])
        bn_off = sb("bn_off", [1])
        shift = sb("shift", [1])
        stats = sb("stats", [CHUNKS * 6])
        mv = sb("mv", [B, 2])
        gmean = sb("gmean", [B])
        dev = sb("dev", [B])
        var = sb("var", [B + 1])
        std = sb("std", [B + 1])
        rstd = sb("rstd", [B + 1])
        newton = sb("newton", [B + 1])
        mean_t = sb("mean_t", [NS])
        rstd_t = sb("rstd_t", [NS])
        xn = sb("xn", [SP])
        hs = sb("hs", [NW, WS, NP])
        ht = sb("ht", [NW, WS])
        vt = sb("vt", [NW, NP])
        xp = sb("xp", [TP * P])
        km = sb("km", [TV, 4, P])
        vm = sb("vm", [TF * WF + TP * WP, 4, VC])
        qm = sb("qm", [4, TV * P])
        kvc = sb("kvc", [2 * NW, KC])
        den = sb("den", [2 * NW, 4])
        rden = sb("rden", [2 * NW, 4])
        rm = sb("rm", [2 * NW, 4])
        num = sb("num", [2 * NW, Q4])
        two = sb("two", [TP * 4, Q4])
        oT = sb("oT", [TV * 4, Q4])
        o_sb = sb("o_sb", [2, SP])

        ps = ctx.enter_context(nc.psum_tensor("ps", [P, 8, 512], F32))
        KVF = 0
        K_F, V_F = 0, 1
        K_P, V_P = 2, 3
        Q_F, Q_P = 2, 3
        KVP = OUTF = 4
        TRF, TRP = 6, 7
        PROJ = 7
        OUTP = 6

        loaded_w = sem("loaded_w")
        loaded_x = [sem(f"loaded_x{i}") for i in range(B * LOADS)]
        dv_setup = sem("dv_setup")
        dv = sem("dv")
        pl = sem("pl")
        pads_zero = sem("pads_zero")
        ones_set = sem("ones_set")
        stat_in = sem("stat_in")
        stat_out = sem("stat_out")
        std_in = sem("std_in")
        std_out = sem("std_out")
        proj_scaled = sem("proj_scaled")
        proj_turned = sem("proj_turned")
        projT_ready = sem("projT_ready")
        xn_ready, xp_ready = sem("xn_ready"), sem("xp_ready")
        k_f, v_f, k_p, v_p = sem("k_f"), sem("v_f"), sem("k_p"), sem("v_p")
        q_f, q_p = sem("q_f"), sem("q_p")
        km_f, km_p = sem("km_f"), sem("km_p")
        vm_f, vm_p = sem("vm_f"), sem("vm_p")
        qm_f, qm_p = sem("qm_f"), sem("qm_p")
        kv_f, kv_p = sem("kv_f"), sem("kv_p")
        kvc_f, kvc_p = sem("kvc_f"), sem("kvc_p")
        out_f, out_p = sem("out_f"), sem("out_p")
        oT_f, oT_p = sem("oT_f"), sem("oT_p")
        tr_f, tr_p = sem("tr_f"), sem("tr_p")
        o_f, o_p = sem("o_f"), sem("o_p")
        projected = sem("projected")
        y_done = sem("y_done")
        stored = sem("stored")

        def col(i, n=1):
            return cst[:, i:i + n]

        def first(s):
            return isinstance(s, int) and s == 0

        block = ctx.enter_context(nc.Block())

        @block.sync
        def _(sp):
            for dst, src in ((cst, consts), (wkv_sb, wkv), (wq_sb, wq), (proj_sb, proj), (bn_sb, bn)):
                sp.dma_start(dst[:], src).then_inc(loaded_w, 16)
            part = HW // LOADS
            for b in range(B):
                for i in range(LOADS):
                    sp.dma_start(x_all[:, b * HW + i * part:b * HW + (i + 1) * part],
                                 x_v[:, b, i * part:(i + 1) * part]).then_inc(loaded_x[b * LOADS + i], 16)
            for b in range(B):
                with sp.Fori(0, SPB) as t:
                    sp.wait_ge(y_done, t + (b * SPB + 1))
                    sp.dma_start(out_v[:, b, bass.ds(t * SP, SP)],
                                 x_all[:, bass.ds(t * SP + b * HW, SP)]).then_inc(stored, 16)
            sp.wait_ge(stored, 16 * NS)

        @block.gpsimd
        def _(pool):
            PL = 6
            pool.memset(xp[:], 0.0).then_inc(pads_zero, 1)

            def add(o, a, b):
                return pool.tensor_tensor(o, a, b, ALU.add)

            def pooling(s):
                xv = xn[:].rearrange("p (w r c) -> p w r c", r=WS, c=WS)
                xo = xp[:].rearrange("p (q j) -> p q j", j=Q4)[:, :, 0:WP * PXP].rearrange(
                    "p q (w r c) -> p q w r c", w=WP, c=NP)
                h3 = hs[:].rearrange("p (q w) r c -> p q w r c", w=WP)
                v3 = vt[:].rearrange("p (q w) c -> p q w c", w=WP)

                def link(ins, n):
                    ins.then_inc(pl, 1)
                    pool.wait_ge(pl, s * PL + n)

                pool.wait_ge(xn_ready, s + 1)
                link(add(ht[:], xv[:, :, :, 1], xv[:, :, :, 2]), 1)
                link(add(hs[:, :, :, 0], ht[:], xv[:, :, :, 0]), 2)
                add(hs[:, :, :, 2], ht[:], xv[:, :, :, 3])
                link(add(hs[:, :, :, 1], hs[:, :, :, 0], xv[:, :, :, 3]), 3)
                link(add(vt[:], hs[:, :, 1, :], hs[:, :, 2, :]), 4)
                if not first(s):
                    pool.wait_ge(q_p, s)
                link(add(xo[:, :, :, 0, :], v3, h3[:, :, :, 0, :]), 5)
                add(xo[:, :, :, 2, :], v3, h3[:, :, :, 3, :]).then_inc(pl, 1)
                add(xo[:, :, :, 1, :], xo[:, :, :, 0, :], h3[:, :, :, 3, :]).then_inc(xp_ready, 1)

            pool.wait_ge(pads_zero, 1)
            pooling(0)
            with pool.Fori(1, NS) as s:
                pooling(s)

        @block.scalar
        def _(act):
            def masked_k(s):
                for ready, free, done, bank, t0, n, mask in (
                        (k_f, kv_f, km_f, K_F, 0, TF, C_QUAD), (k_p, kv_p, km_p, K_P, TF, TP, C_QUADP)):
                    act.wait_ge(ready, s + 1)
                    if not first(s):
                        act.wait_ge(free, s)
                    for r in range(4):
                        last = act.activation(km[:, t0:t0 + n, r, :],
                                              ps[:, bank, 0:n * P].rearrange("p (t c) -> p t c", c=P),
                                              ACT.Relu, scale=col(mask + r))
                    last.then_inc(done, 1)

            def masked_q(s):
                for ready, free, done, bank, t0, n, mask in (
                        (q_f, out_f, qm_f, Q_F, 0, TF, C_QUAD), (q_p, out_p, qm_p, Q_P, TF, TP, C_QUADP)):
                    act.wait_ge(ready, s + 1)
                    if not first(s):
                        act.wait_ge(free, s)
                    for i in range(4):
                        last = act.activation(qm[:, i, t0 * P:(t0 + n) * P], ps[:, bank, 0:n * P],
                                              ACT.Relu, scale=col(mask + i))
                    last.then_inc(done, 1)

            def to_image(s):
                o_v = o_sb[:].rearrange("p z (r w c) -> p z w r c", r=WS, c=WS)
                act.wait_ge(tr_f, s + 1)
                if not first(s):
                    act.wait_ge(projected, s)
                act.activation(o_v[:, 0], ps[:, TRF, 0:SP].rearrange("p (w r c) -> p w r c", r=WS, c=WS),
                               ACT.Copy).then_inc(o_f, 1)
                act.wait_ge(tr_p, s + 1)
                src = ps[:, TRP, 0:TP * P].rearrange("p (q j) -> p q j", j=Q4)[:, :, 0:WP * PXP].rearrange(
                    "p q (w r c) -> p q w r c", w=WP, c=NP)
                dst = o_v[:, 1].rearrange("p (q w) r c -> p q w r c", w=WP)
                shape = [P, TP * 4, WP, 2]
                for r in range(WS):
                    rr = (0, 1, 1, 2)[r]
                    act.activation(dst[:, :, :, r, 0:4:3], src[:, :, :, rr, 0:3:2], ACT.Copy)
                    last = act.activation(dst[:, :, :, r, 1:3], src[:, :, :, rr, 1:2].to_broadcast(shape),
                                          ACT.Copy)
                last.then_inc(o_p, 1)

            act.wait_ge(std_in, 1)
            act.activation(std[:], var[:], ACT.Sqrt).then_inc(std_out, 1)
            act.wait_ge(loaded_w, 16 * 5)
            masked_k(0)
            masked_q(0)
            masked_k(1)
            masked_q(1)

            def step(s):
                to_image(s - 1)
                masked_k(s + 1)
                masked_q(s + 1)

            step(1)
            with act.Fori(2, NS - 1) as s:
                step(s)
            to_image(NS - 2)
            to_image(NS - 1)

        @block.vector
        def _(dve):
            count = [0]
            DV = 9

            def setup(ins):
                count[0] += 1
                ins.then_inc(dv_setup, 1)
                dve.wait_ge(dv_setup, count[0])

            part = CHUNKS // LOADS
            for b in range(B):
                for c in range(CHUNKS):
                    if c % part == 0:
                        dve.wait_ge(loaded_x[b * LOADS + c // part], 16)
                    last = dve.bn_stats(stats[:, 6 * c:6 * c + 6],
                                        x_all[:, b * HW + c * STAT:b * HW + (c + 1) * STAT])
                setup(last)
                setup(dve.bn_aggr(mv[:, b, :], stats[:]))
            dve.tensor_copy(dev[:], mv[:, :, 0]).then_inc(stat_in, 1)
            dve.wait_ge(stat_out, 1)
            setup(dve.tensor_copy(gmean[:], ps[:, 6, 0:B]))
            setup(dve.tensor_tensor(dev[:], mv[:, :, 0], gmean[:], ALU.subtract))
            setup(dve.tensor_tensor(dev[:], dev[:], dev[:], ALU.mult))
            setup(dve.tensor_tensor(dev[:], dev[:], mv[:, :, 1], ALU.add))
            dve.tensor_copy(var[:, 0:B], dev[:]).then_inc(stat_in, 1)
            dve.wait_ge(stat_out, 2)
            dve.wait_ge(loaded_w, 16 * 5)
            dve.tensor_scalar(var[:, 0:B], ps[:, 7, 0:B], GN_EPS, None, ALU.add)
            dve.tensor_scalar(var[:, B:B + 1], bn_sb[:, 3:4], BN_EPS, None, ALU.add).then_inc(std_in, 1)
            dve.wait_ge(std_out, 1)
            setup(dve.reciprocal(rstd[:], std[:]))
            setup(dve.tensor_tensor(newton[:], rstd[:], rstd[:], ALU.mult))
            setup(dve.tensor_tensor(newton[:], newton[:], var[:], ALU.mult))
            setup(dve.tensor_scalar(newton[:], newton[:], -0.5, 1.5, ALU.mult, ALU.add))
            setup(dve.tensor_tensor(rstd[:], rstd[:], newton[:], ALU.mult))
            setup(dve.tensor_tensor(bn_inv[:], bn_sb[:, 0:1], rstd[:, B:B + 1], ALU.mult))
            setup(dve.tensor_tensor(bn_off[:], bn_sb[:, 2:3], bn_inv[:], ALU.mult))
            setup(dve.tensor_tensor(shift[:], bn_sb[:, 1:2], bn_off[:], ALU.subtract))
            dve.tensor_scalar(proj_sb[:], proj_sb[:], bn_inv[:], None, ALU.mult).then_inc(proj_scaled, 1)
            for b in range(B):
                dve.tensor_copy(mean_t[:, b * SPB:(b + 1) * SPB], gmean[:, b:b + 1].to_broadcast([P, SPB]))
                last = dve.tensor_copy(rstd_t[:, b * SPB:(b + 1) * SPB],
                                       rstd[:, b:b + 1].to_broadcast([P, SPB]))
            setup(last)
            for n0, tiles, wins, mask in ((0, TF, WF, C_WF), (TF * WF, TP, WP, C_WPM)):
                for e in range(wins):
                    last = dve.tensor_copy(vm[:, n0 + e:n0 + tiles * wins:wins, :, Q4],
                                           col(mask + e).unsqueeze(2).to_broadcast([P, tiles, 4]))
            last.then_inc(ones_set, 1)
            dve.wait_ge(proj_turned, 1)
            dve.tensor_copy(projT[:], ps[:, 7, 0:2 * P]).then_inc(projT_ready, 1)

            def link(ins, s, n):
                ins.then_inc(dv, 1)
                dve.wait_ge(dv, s * DV + n)

            def normalise(s):
                if not first(s):
                    dve.wait_ge(q_p, s)
                    dve.wait_ge(xp_ready, s)
                dst = xn[:].rearrange("p (w r c) -> p r w c", r=WS, c=WS)
                src = x_all[:, bass.ds(s * SP, SP)].rearrange("p (r w c) -> p r w c", r=WS, c=WS)
                dve.tensor_scalar(dst, src, mean_t[:, bass.ds(s, 1)], rstd_t[:, bass.ds(s, 1)],
                                  ALU.subtract, ALU.mult).then_inc(xn_ready, 1)

            def masked_v(s):
                for ready, free, done, bank, n0, tiles, wins, mask in (
                        (v_f, kv_f, vm_f, V_F, 0, TF, WF, C_WF),
                        (v_p, kv_p, vm_p, V_P, TF * WF, TP, WP, C_WPV)):
                    dve.wait_ge(ready, s + 1)
                    if not first(s):
                        dve.wait_ge(free, s)
                    for e in range(wins):
                        last = dve.tensor_scalar(
                            vm[:, n0 + e:n0 + tiles * wins:wins, :, 0:Q4],
                            ps[:, bank, 0:tiles * P].rearrange("p (t i c) -> p t i c", i=4, c=Q4),
                            col(mask + e), None, ALU.mult)
                    last.then_inc(done, 1)

            def own_heads(s):
                for ready, free, done, bank, w0 in ((kv_f, out_f, kvc_f, KVF, 0), (kv_p, out_p, kvc_p, KVP, NW)):
                    dve.wait_ge(ready, s + 1)
                    if not first(s):
                        dve.wait_ge(free, s)
                    src = ps[:, bank:bank + 2, 0:HALF * VC].rearrange("p b (w c) -> p b w c", c=VC)
                    dst = kvc[:, w0:w0 + NW, :].rearrange("p (b w) c -> p b w c", b=2)
                    for b in range(2):
                        dve.tensor_tensor(dst[:, b, :, 0:Q4], src[:, b, :, 0:Q4],
                                          col(C_HEAD, Q4).unsqueeze(1).to_broadcast([P, HALF, Q4]), ALU.mult)
                        last = dve.tensor_tensor(
                            dst[:, b, :, Q4:KC], src[:, b, :, Q4:VC].to_broadcast([P, HALF, 4]),
                            col(C_HEAD + Q4, 4).unsqueeze(1).to_broadcast([P, HALF, 4]), ALU.mult)
                    last.then_inc(done, 1)

            def divide(s, pooled):
                ready, free, done, bank, w0, wins, mask, step = (
                    (out_p, tr_p, oT_p, OUTP, NW, WP, C_WP, 4) if pooled else
                    (out_f, tr_f, oT_f, OUTF, 0, WF, C_WF, 0))
                chunks = NW // wins
                dve.wait_ge(ready, s + 1)
                src = ps[:, bank:bank + 2, 0:HALF * KC].rearrange("p b (w c) -> p b w c", c=KC)
                d, rd, r = (t[:, w0:w0 + NW, :] for t in (den, rden, rm))
                nm = num[:, w0:w0 + NW, :]
                link(dve.tensor_scalar(d.rearrange("p (b w) h -> p b w h", b=2), src[:, :, :, Q4:KC],
                                       DEN_EPS, None, ALU.add), s, step + 1)
                link(dve.reciprocal(rd, d), s, step + 2)
                link(dve.tensor_tensor(
                    r.rearrange("p (k e) h -> p k e h", e=wins), rd.rearrange("p (k e) h -> p k e h", e=wins),
                    col(mask, wins).unsqueeze(1).unsqueeze(3).to_broadcast([P, chunks, wins, 4]),
                    ALU.mult), s, step + 3)
                for b in range(2):
                    h = slice(b * HALF, (b + 1) * HALF)
                    last = dve.tensor_tensor(
                        nm[:, h, :].rearrange("p w (h m) -> p w h m", m=D),
                        src[:, b, :, 0:Q4].rearrange("p w (h m) -> p w h m", m=D),
                        r[:, h, :].unsqueeze(3).to_broadcast([P, HALF, 4, D]), ALU.mult)
                link(last, s, step + 4)
                if not first(s):
                    dve.wait_ge(free, s)
                ne = nm.rearrange("p (k e) c -> p k e c", e=wins)
                if pooled:
                    link(dve.tensor_tensor(two[:], ne[:, :, 0], ne[:, :, 1], ALU.add), s, step + 5)
                    dve.tensor_tensor(oT[:, TF * 4:TV * 4, :], two[:], ne[:, :, 2], ALU.add).then_inc(done, 1)
                else:
                    dve.tensor_tensor(oT[:, 0:TF * 4, :], ne[:, :, 0], ne[:, :, 1], ALU.add).then_inc(done, 1)

            def residual(s):
                dve.wait_ge(projected, s + 1)
                xs = x_all[:, bass.ds(s * SP, SP)]
                dve.scalar_tensor_tensor(xs, ps[:, PROJ, 0:SP], shift[:], xs, ALU.add,
                                         ALU.add).then_inc(y_done, 1)

            normalise(0)
            masked_v(0)
            normalise(1)
            own_heads(0)
            masked_v(1)

            def step(s):
                divide(s - 1, False)
                normalise(s + 1)
                divide(s - 1, True)
                own_heads(s)
                masked_v(s + 1)
                residual(s - 1)

            step(1)
            with dve.Fori(2, NS - 1) as s:
                step(s)
            divide(NS - 2, False)
            divide(NS - 2, True)
            own_heads(NS - 1)
            residual(NS - 2)
            divide(NS - 1, False)
            divide(NS - 1, True)
            residual(NS - 1)

        @block.tensor
        def _(pe):
            pe.wait_ge(loaded_w, 16 * 5)
            pe.wait_ge(stat_in, 1)
            pe.matmul(ps[:, 6, 0:B], col(C_GROUP, P), dev[:], start=True, stop=True).then_inc(stat_out, 1)
            pe.wait_ge(stat_in, 2)
            pe.matmul(ps[:, 7, 0:B], col(C_GROUP, P), var[:, 0:B], start=True, stop=True).then_inc(stat_out, 1)
            pe.wait_ge(proj_scaled, 1)
            for z in range(2):
                last = pe.transpose(ps[:, 7, z * P:(z + 1) * P], proj_sb[:, z * P:(z + 1) * P], col(C_IDENT, P))
            last.then_inc(proj_turned, 1)
            pe.wait_ge(projT_ready, 1)
            pe.wait_ge(ones_set, 1)

            def conv_kv(s):
                pe.wait_ge(xn_ready, s + 1)
                if not first(s):
                    pe.wait_ge(kvc_f, s)
                for half, bank, done in ((0, K_F, k_f), (1, V_F, v_f)):
                    for t in range(TF):
                        last = pe.matmul(ps[:, bank, t * P:(t + 1) * P], xn[:, t * P:(t + 1) * P],
                                         wkv_sb[:, half * P:(half + 1) * P], start=True, stop=True)
                    last.then_inc(done, 1)
                pe.wait_ge(xp_ready, s + 1)
                if not first(s):
                    pe.wait_ge(qm_f, s)
                    pe.wait_ge(qm_p, s)
                for half, bank, done in ((0, K_P, k_p), (1, V_P, v_p)):
                    for t in range(TP):
                        last = pe.matmul(ps[:, bank, t * P:(t + 1) * P], xp[:, t * P:(t + 1) * P],
                                         wkv_sb[:, half * P:(half + 1) * P], start=True, stop=True)
                    last.then_inc(done, 1)

            def conv_q(s):
                pe.wait_ge(km_p, s + 1)
                pe.matmul(ps[:, Q_F, 0:SP], wq_sb[:], xn[:], start=True, stop=True).then_inc(q_f, 1)
                pe.wait_ge(vm_p, s + 1)
                pe.matmul(ps[:, Q_P, 0:TP * P], wq_sb[:], xp[:], start=True, stop=True).then_inc(q_p, 1)

            def kv_products(s):
                pe.wait_ge(km_f, s + 1)
                pe.wait_ge(vm_f, s + 1)
                for t in range(TF):
                    for r in range(4):
                        b, at = divmod((t * 4 + r) * WF, HALF)
                        for i in range(4):
                            last = pe.matmul(ps[Q4 * i:Q4 * (i + 1), KVF + b, at * VC:(at + WF) * VC],
                                             km[:, t, r, Q4 * i:Q4 * (i + 1)],
                                             vm[:, t * WF:(t + 1) * WF, i, :], start=True, stop=True)
                last.then_inc(kv_f, 1)
                pe.wait_ge(km_p, s + 1)
                pe.wait_ge(vm_p, s + 1)
                if not first(s):
                    pe.wait_ge(oT_f, s)
                for t in range(TP):
                    for r in range(4):
                        b, at = divmod((t * 4 + r) * WP, HALF)
                        for i in range(4):
                            last = pe.matmul(ps[Q4 * i:Q4 * (i + 1), KVP + b, at * VC:(at + WP) * VC],
                                             km[:, TF + t, r, Q4 * i:Q4 * (i + 1)],
                                             vm[:, TF * WF + t * WP:TF * WF + (t + 1) * WP, i, :],
                                             start=True, stop=True)
                last.then_inc(kv_p, 1)

            def out_products(s):
                pe.wait_ge(qm_f, s + 1)
                pe.wait_ge(kvc_f, s + 1)
                pe.wait_ge(kvc_p, s + 1)
                for t in range(TF):
                    for i in range(4):
                        b, at = divmod((t * 4 + i) * WF, HALF)
                        for c in range(4):
                            w = (t * 4 + c) * WF
                            last = pe.matmul(ps[Q4 * c:Q4 * (c + 1), OUTF + b, at * KC:(at + WF) * KC],
                                             qm[:, i, t * P + Q4 * c:t * P + Q4 * (c + 1)],
                                             kvc[:, w:w + WF, :], start=True, stop=True)
                last.then_inc(out_f, 1)
                pe.wait_ge(qm_p, s + 1)
                if not first(s):
                    pe.wait_ge(o_f, s)
                    pe.wait_ge(y_done, s)
                for t in range(TP):
                    for i in range(4):
                        b, at = divmod((t * 4 + i) * WP, HALF)
                        for c in range(4):
                            w = NW + (t * 4 + c) * WP
                            last = pe.matmul(ps[Q4 * c:Q4 * (c + 1), OUTP + b, at * KC:(at + WP) * KC],
                                             qm[:, i, (TF + t) * P + Q4 * c:(TF + t) * P + Q4 * (c + 1)],
                                             kvc[:, w:w + WP, :], start=True, stop=True)
                last.then_inc(out_p, 1)

            def transposes(s):
                pe.wait_ge(oT_f, s + 1)
                pe.wait_ge(oT_p, s + 1)
                for bank, t0, n, done in ((TRF, 0, TF, tr_f), (TRP, TF, TP, tr_p)):
                    for t in range(n):
                        last = pe.transpose(
                            ps[:, bank, t * P:(t + 1) * P],
                            oT[:, (t0 + t) * 4:(t0 + t + 1) * 4, :].rearrange("p i c -> p (i c)"),
                            col(C_IDENT, P))
                    last.then_inc(done, 1)

            def project(s):
                pe.wait_ge(o_f, s + 1)
                pe.wait_ge(o_p, s + 1)
                pe.matmul(ps[:, PROJ, 0:SP], projT[:, 0:P], o_sb[:, 0, :], start=True, stop=False)
                pe.matmul(ps[:, PROJ, 0:SP], projT[:, P:2 * P], o_sb[:, 1, :], start=False,
                          stop=True).then_inc(projected, 1)

            conv_kv(0)
            conv_q(0)
            kv_products(0)
            conv_kv(1)
            out_products(0)
            conv_q(1)
            with pe.Fori(1, NS - 1) as s:
                kv_products(s)
                transposes(s - 1)
                conv_kv(s + 1)
                project(s - 1)
                out_products(s)
                conv_q(s + 1)
            kv_products(NS - 1)
            transposes(NS - 2)
            project(NS - 2)
            out_products(NS - 1)
            transposes(NS - 1)
            project(NS - 1)


def kernel(x, L0_conv_qkv_w, L0_conv_proj_w, L0_conv_bn_gamma, L0_conv_bn_beta, L0_conv_bn_mean,
           L0_conv_bn_var):
    import concourse.bacc as bacc
    from concourse.bass_utils import run_bass_kernel_spmd

    heads = P // D
    w = np.asarray(L0_conv_qkv_w).reshape(heads, 3, D, P).transpose(1, 3, 0, 2).reshape(3, P, P)
    arrays = {
        "x": np.ascontiguousarray(x),
        "wq": np.ascontiguousarray(w[0]),
        "wkv": np.ascontiguousarray(np.concatenate([w[1], w[2]], axis=1)),
        "proj": np.ascontiguousarray(L0_conv_proj_w),
        "bn": np.stack([np.asarray(a) for a in (L0_conv_bn_gamma, L0_conv_bn_beta, L0_conv_bn_mean,
                                                L0_conv_bn_var)], axis=1),
        "consts": constants(),
    }
    nc = bacc.Bacc("TRN2", target_bir_lowering=False, num_devices=1)
    aps = {n: nc.dram_tensor(n, a.shape, mybir.dt.from_np(a.dtype), kind="ExternalInput").ap()
           for n, a in arrays.items()}
    out = nc.dram_tensor("out", arrays["x"].shape, F32, kind="ExternalOutput").ap()
    build(nc, **aps, out=out)
    r = run_bass_kernel_spmd(nc, [arrays], core_ids=[0])
    return r.results[0]["out"]
```

```python
from contextlib import ExitStack

import numpy as np

import concourse.bass as bass
from concourse import mybir

F32 = mybir.dt.float32
ALU = mybir.AluOpType
ACT = mybir.ActivationFunctionType

P = 128
Q4 = 32
WS = 4
D = 8
GROUPS = 32
GN_EPS, BN_EPS, DEN_EPS = 1e-5, 1e-5, 1e-15

PX = WS * WS
PXP = 9
NP = WS - 1
WF = Q4 // PX
WP = Q4 // PXP
VC = Q4 + 1
KC = Q4 + 4
G = 2
QG = 4 // G

C_IDENT, C_GROUP = 0, P
C_HEAD = 2 * P
C_HALF = C_HEAD + QG * KC
C_HALFP = C_HALF + G
C_VF = C_HALFP + G
C_VP = C_VF + QG * WF
C_OF = C_VP + QG * WP
C_OP = C_OF + QG * WF
C_WF = C_OP + QG * WP
C_WP = C_WF + WF
C_PACK = C_WP + WP
N_CONST = C_PACK + P


def constants():
    c = np.zeros((P, N_CONST), np.float32)
    p = np.arange(P)
    c[:, C_IDENT:C_IDENT + P] = np.eye(P)
    per = P // GROUPS
    c[:, C_GROUP:C_GROUP + P] = (p[:, None] // per == p[None] // per) / per
    quad, head = p // Q4, p % Q4 // D
    for j in range(QG):
        at = C_HEAD + j * KC
        mine = quad[:, None] % QG == j
        c[:, at:at + Q4] = mine & (head[:, None] == np.arange(Q4)[None] // D)
        c[:, at + Q4:at + KC] = mine & (head[:, None] == np.arange(4)[None])
    half = quad[:, None] // QG == np.arange(G)[None]
    c[:, C_HALF:C_HALF + G] = half
    c[:, C_HALFP:C_HALFP + G] = half / 25.0
    win_f, win_p = p % Q4 // PX, p % Q4 // PXP
    side = np.array([1, 2, 1])
    times = (side[:, None] * side[None]).ravel()[p % Q4 % PXP][:, None]
    own_f = (quad % QG * WF + win_f)[:, None] == np.arange(QG * WF)[None]
    own_p = ((quad % QG * WP + win_p)[:, None] == np.arange(QG * WP)[None]) & (win_p < WP)[:, None]
    c[:, C_VF:C_VF + QG * WF] = own_f
    c[:, C_VP:C_VP + QG * WP] = own_p * times / 25.0
    c[:, C_OF:C_OF + QG * WF] = own_f
    c[:, C_OP:C_OP + QG * WP] = own_p * times
    c[:, C_WF:C_WF + WF] = win_f[:, None] == np.arange(WF)[None]
    c[:, C_WP:C_WP + WP] = win_p[:, None] == np.arange(WP)[None]
    pads = p % Q4 >= WP * PXP
    c[np.concatenate([p[~pads], p[pads]]), C_PACK + p] = 1
    return c


def build(nc, x, wq, wkv, proj, bn, consts, out):
    B, C, H, W = x.shape
    assert C == P
    HW = H * W
    SPB = H // WS
    NS = B * SPB
    SP = WS * W
    NW = W // WS
    TF = SP // P
    TP = NW // (4 * WP)
    assert TF * P == SP and TP * 4 * WP == NW
    HALF = NW // 2
    assert HALF * KC <= 512
    VF, VP = QG * WF, QG * WP
    TV = TF + TP
    STAT = 512
    CHUNKS = HW // STAT
    LOADS = 3
    assert CHUNKS % LOADS == 0

    x_v = x.rearrange("b c h w -> c b (h w)")
    out_v = out.rearrange("b c h w -> c b (h w)")

    with ExitStack() as ctx:
        def sb(name, shape):
            return ctx.enter_context(nc.sbuf_tensor(name, [P, *shape], F32))

        def sem(name):
            return ctx.enter_context(nc.semaphore(name))

        x_all = sb("x_all", [NS * SP])
        cst = sb("cst", [N_CONST])
        wq_sb = sb("wq_sb", [P])
        wkv_sb = sb("wkv_sb", [2 * P])
        projT = sb("projT", [2 * P])
        bn_sb = sb("bn_sb", [4])
        bn_inv = sb("bn_inv", [1])
        bn_off = sb("bn_off", [1])
        shift = sb("shift", [1])
        stats = sb("stats", [CHUNKS * 6])
        mv = sb("mv", [B, 2])
        gmean = sb("gmean", [B])
        dev = sb("dev", [B])
        var = sb("var", [B + 1])
        std = sb("std", [B + 1])
        rstd = sb("rstd", [B + 1])
        newton = sb("newton", [B + 1])
        mean_t = sb("mean_t", [NS])
        rstd_t = sb("rstd_t", [NS])
        xn = sb("xn", [2, SP])
        hs = sb("hs", [NW, WS, NP])
        ht = sb("ht", [NW, WS])
        vt = sb("vt", [NW, NP])
        xp = sb("xp", [2, TP * P])
        km = sb("km", [TV, G, P])
        vm = sb("vm", [TF * VF + TP * VP, 4, VC])
        qm = sb("qm", [G, TV * P])
        kvc = sb("kvc", [2 * NW, QG, KC])
        rm = sb("rm", [2 * NW, 4])
        num = sb("num", [2 * NW, Q4])
        two = sb("two", [TP * G, QG * Q4])
        oT = sb("oT", [TV * G, QG * Q4])
        o_sb = sb("o_sb", [2, SP])
        proj_sb = o_sb[:].rearrange("p z x -> p (z x)")[:, 0:2 * P]

        ps = ctx.enter_context(nc.psum_tensor("ps", [P, 8, 512], F32))
        KVF = 0
        TRF, TRP, PROJ = 0, 1, 1
        K_F, V_F = 2, 3
        OUTP = 2
        KVP = 4
        OUTF = 4
        K_P, V_P = 6, 7
        Q_F, Q_P = 6, 7

        loaded_w = sem("loaded_w")
        loaded_x = [sem(f"loaded_x{i}") for i in range(B * LOADS)]
        dv_setup = sem("dv_setup")
        dv = sem("dv")
        pl = sem("pl")
        pads_zero = sem("pads_zero")
        ones_set = sem("ones_set")
        stat_in = sem("stat_in")
        stat_out = sem("stat_out")
        std_in = sem("std_in")
        std_out = sem("std_out")
        proj_scaled = sem("proj_scaled")
        proj_turned = sem("proj_turned")
        projT_ready = sem("projT_ready")
        xn_ready, xp_ready = sem("xn_ready"), sem("xp_ready")
        k_f, v_f, k_p, v_p = sem("k_f"), sem("v_f"), sem("k_p"), sem("v_p")
        q_f, q_p = sem("q_f"), sem("q_p")
        km_f, km_p = sem("km_f"), sem("km_p")
        vm_f, vm_p = sem("vm_f"), sem("vm_p")
        qm_f, qm_p = sem("qm_f"), sem("qm_p")
        kv_f, kv_p = sem("kv_f"), sem("kv_p")
        kvc_f, kvc_p = sem("kvc_f"), sem("kvc_p")
        out_f, out_p = sem("out_f"), sem("out_p")
        num_f, num_p = sem("num_f"), sem("num_p")
        two_ready = sem("two_ready")
        oT_f, oT_p = sem("oT_f"), sem("oT_p")
        tr_f, tr_p = sem("tr_f"), sem("tr_p")
        o_f, o_p = sem("o_f"), sem("o_p")
        projected = sem("projected")
        y_done = sem("y_done")
        stored = sem("stored")

        def col(i, n=1):
            return cst[:, i:i + n]

        def wait(eng, semaphore, value):
            if not (isinstance(value, int) and value <= 0):
                eng.wait_ge(semaphore, value)

        def over_strips(eng, step):
            for s in (0, 1, 2):
                step(s, s % 2)
            with eng.Fori(3, NS - 3, 2) as s:
                step(s, 1)
                step(s + 1, 0)
            for s in (NS - 3, NS - 2, NS - 1):
                step(s, s % 2)

        def is_last(s):
            return isinstance(s, int) and s == NS - 1

        def is_first(s):
            return isinstance(s, int) and s == 0

        block = ctx.enter_context(nc.Block())

        @block.sync
        def _(sp):
            for dst, src in ((cst, consts), (wkv_sb, wkv), (wq_sb, wq), (proj_sb, proj), (bn_sb, bn)):
                sp.dma_start(dst if dst is proj_sb else dst[:], src).then_inc(loaded_w, 16)
            part = HW // LOADS
            for b in range(B):
                for i in range(LOADS):
                    sp.dma_start(x_all[:, b * HW + i * part:b * HW + (i + 1) * part],
                                 x_v[:, b, i * part:(i + 1) * part]).then_inc(loaded_x[b * LOADS + i], 16)
            for b in range(B):
                with sp.Fori(0, SPB) as t:
                    sp.wait_ge(y_done, t + (b * SPB + 1))
                    sp.dma_start(out_v[:, b, bass.ds(t * SP, SP)],
                                 x_all[:, bass.ds(t * SP + b * HW, SP)]).then_inc(stored, 16)
            sp.wait_ge(stored, 16 * NS)

        @block.gpsimd
        def _(pool):
            PL = 6
            pool.memset(xp[:], 0.0).then_inc(pads_zero, 1)
            pool.memset(qm[:], 0.0).then_inc(pads_zero, 1)

            def add(o, a, b):
                return pool.tensor_tensor(o, a, b, ALU.add)

            def pooling(s, p):
                xv = xn[:, p].rearrange("p (w r c) -> p w r c", r=WS, c=WS)
                xo = xp[:, p].rearrange("p (q j) -> p q j", j=Q4)[:, :, 0:WP * PXP].rearrange(
                    "p q (w r c) -> p q w r c", w=WP, c=NP)
                h3 = hs[:].rearrange("p (q w) r c -> p q w r c", w=WP)
                v3 = vt[:].rearrange("p (q w) c -> p q w c", w=WP)

                def link(ins, n):
                    ins.then_inc(pl, 1)
                    pool.wait_ge(pl, s * PL + n)

                pool.wait_ge(xn_ready, s + 1)
                link(add(ht[:], xv[:, :, :, 1], xv[:, :, :, 2]), 1)
                link(add(hs[:, :, :, 0], ht[:], xv[:, :, :, 0]), 2)
                add(hs[:, :, :, 2], ht[:], xv[:, :, :, 3])
                link(add(hs[:, :, :, 1], hs[:, :, :, 0], xv[:, :, :, 3]), 3)
                link(add(vt[:], hs[:, :, 1, :], hs[:, :, 2, :]), 4)
                wait(pool, q_p, s - 1)
                link(add(xo[:, :, :, 0, :], v3, h3[:, :, :, 0, :]), 5)
                add(xo[:, :, :, 2, :], v3, h3[:, :, :, 3, :]).then_inc(pl, 1)
                add(xo[:, :, :, 1, :], xo[:, :, :, 0, :], h3[:, :, :, 3, :]).then_inc(xp_ready, 1)

            pool.wait_ge(pads_zero, 2)

            def own_window(s):
                nf = num[:, 0:NW].rearrange("p (k e j) c -> p k e (j c)", e=WF, j=QG)
                np_ = num[:, NW:2 * NW].rearrange("p (k e j) c -> p k e (j c)", e=WP, j=QG)
                pool.wait_ge(num_f, s + 1)
                wait(pool, tr_f, s)
                add(oT[:, 0:TF * G, :], nf[:, :, 0], nf[:, :, 1]).then_inc(oT_f, 1)
                pool.wait_ge(num_p, s + 1)
                add(two[:], np_[:, :, 0], np_[:, :, 1]).then_inc(two_ready, 1)
                wait(pool, tr_p, s)
                pool.wait_ge(two_ready, s + 1)
                add(oT[:, TF * G:TV * G, :], two[:], np_[:, :, 2]).then_inc(oT_p, 1)

            def step(s, p):
                if not isinstance(s, int) or s < NS - 2:
                    pooling(s + 2, p)
                own_window(s)

            pooling(0, 0)
            pooling(1, 1)
            over_strips(pool, step)

        @block.scalar
        def _(act):
            def masked_k(s, pooled):
                ready, free, done, bank, t0, n, mask = (
                    (k_p, kv_p, km_p, K_P, TF, TP, C_HALFP) if pooled else (k_f, kv_f, km_f, K_F, 0, TF, C_HALF))
                act.wait_ge(ready, s + 1)
                wait(act, free, s)
                for g in range(G):
                    last = act.activation(km[:, t0:t0 + n, g, :],
                                          ps[:, bank, 0:n * P].rearrange("p (t c) -> p t c", c=P),
                                          ACT.Relu, scale=col(mask + g))
                last.then_inc(done, 1)

            def masked_v(s, pooled):
                ready, free, done, bank, n0, tiles, wins, mask = (
                    (v_p, kv_p, vm_p, V_P, TF * VF, TP, VP, C_VP) if pooled else
                    (v_f, kv_f, vm_f, V_F, 0, TF, VF, C_VF))
                act.wait_ge(ready, s + 1)
                wait(act, free, s)
                for j in range(wins):
                    last = act.activation(
                        vm[:, n0 + j:n0 + tiles * wins:wins, :, 0:Q4],
                        ps[:, bank, 0:tiles * P].rearrange("p (t i c) -> p t i c", i=4, c=Q4),
                        ACT.Copy, scale=col(mask + j))
                last.then_inc(done, 1)

            def masked_q(s):
                for ready, free, done, bank, at, used, n, mask in (
                        (q_f, out_f, qm_f, Q_F, 0, Q4, TF * 4, C_HALF),
                        (q_p, out_p, qm_p, Q_P, TF * P, WP * PXP, TP * 4, C_HALFP)):
                    act.wait_ge(ready, s + 1)
                    wait(act, free, s)
                    for i in range(G):
                        last = act.activation(
                            qm[:, i, at:at + n * Q4].rearrange("p (q j) -> p q j", j=Q4)[:, :, 0:used],
                            ps[:, bank, 0:n * used].rearrange("p (q j) -> p q j", j=used),
                            ACT.Relu, scale=col(mask + i))
                    last.then_inc(done, 1)

            def to_image(s):
                o_v = o_sb[:].rearrange("p z (r w c) -> p z w r c", r=WS, c=WS)
                act.wait_ge(tr_f, s + 1)
                wait(act, projected, s)
                act.activation(o_v[:, 0], ps[:, TRF, 0:SP].rearrange("p (w r c) -> p w r c", r=WS, c=WS),
                               ACT.Copy).then_inc(o_f, 1)
                act.wait_ge(tr_p, s + 1)
                src = ps[:, TRP, 0:NW * PXP].rearrange("p (w r c) -> p w r c", r=NP, c=NP)
                dst = o_v[:, 1]
                ends, ends_p, mid, mid_p = slice(0, WS, WS - 1), slice(0, NP, NP - 1), slice(1, 3), slice(1, 2)
                for rows, rows_p in ((ends, ends_p), (mid, mid_p)):
                    for cols, cols_p in ((ends, ends_p), (mid, mid_p)):
                        last = act.activation(dst[:, :, rows, cols],
                                              src[:, :, rows_p, cols_p].to_broadcast([P, NW, 2, 2]), ACT.Copy)
                last.then_inc(o_p, 1)

            act.wait_ge(std_in, 1)
            act.activation(std[:], var[:], ACT.Sqrt).then_inc(std_out, 1)
            act.wait_ge(loaded_w, 16 * 5)
            act.wait_ge(pads_zero, 2)

            def step(s, p):
                masked_q(s)
                if not is_last(s):
                    masked_k(s + 1, False)
                    masked_v(s + 1, False)
                if not is_first(s):
                    to_image(s - 1)
                if not is_last(s):
                    masked_k(s + 1, True)
                    masked_v(s + 1, True)

            for pooled in (False, True):
                masked_k(0, pooled)
                masked_v(0, pooled)
            over_strips(act, step)
            to_image(NS - 1)

        @block.vector
        def _(dve):
            count = [0]
            DV = 6

            def setup(ins):
                count[0] += 1
                ins.then_inc(dv_setup, 1)
                dve.wait_ge(dv_setup, count[0])

            part = CHUNKS // LOADS
            for b in range(B):
                for c in range(CHUNKS):
                    if c % part == 0:
                        dve.wait_ge(loaded_x[b * LOADS + c // part], 16)
                    last = dve.bn_stats(stats[:, 6 * c:6 * c + 6],
                                        x_all[:, b * HW + c * STAT:b * HW + (c + 1) * STAT])
                setup(last)
                setup(dve.bn_aggr(mv[:, b, :], stats[:]))
            dve.tensor_copy(dev[:], mv[:, :, 0]).then_inc(stat_in, 1)
            dve.wait_ge(stat_out, 1)
            setup(dve.tensor_copy(gmean[:], ps[:, 6, 0:B]))
            setup(dve.tensor_tensor(dev[:], mv[:, :, 0], gmean[:], ALU.subtract))
            setup(dve.tensor_tensor(dev[:], dev[:], dev[:], ALU.mult))
            setup(dve.tensor_tensor(dev[:], dev[:], mv[:, :, 1], ALU.add))
            dve.tensor_copy(var[:, 0:B], dev[:]).then_inc(stat_in, 1)
            dve.wait_ge(stat_out, 2)
            dve.wait_ge(loaded_w, 16 * 5)
            dve.tensor_scalar(var[:, 0:B], ps[:, 7, 0:B], GN_EPS, None, ALU.add)
            dve.tensor_scalar(var[:, B:B + 1], bn_sb[:, 3:4], BN_EPS, None, ALU.add).then_inc(std_in, 1)
            dve.wait_ge(std_out, 1)
            setup(dve.reciprocal(rstd[:], std[:]))
            setup(dve.tensor_tensor(newton[:], rstd[:], rstd[:], ALU.mult))
            setup(dve.tensor_tensor(newton[:], newton[:], var[:], ALU.mult))
            setup(dve.tensor_scalar(newton[:], newton[:], -0.5, 1.5, ALU.mult, ALU.add))
            setup(dve.tensor_tensor(rstd[:], rstd[:], newton[:], ALU.mult))
            setup(dve.tensor_tensor(bn_inv[:], bn_sb[:, 0:1], rstd[:, B:B + 1], ALU.mult))
            setup(dve.tensor_tensor(bn_off[:], bn_sb[:, 2:3], bn_inv[:], ALU.mult))
            setup(dve.tensor_tensor(shift[:], bn_sb[:, 1:2], bn_off[:], ALU.subtract))
            dve.tensor_scalar(proj_sb, proj_sb, bn_inv[:], None, ALU.mult).then_inc(proj_scaled, 1)
            for b in range(B):
                dve.tensor_copy(mean_t[:, b * SPB:(b + 1) * SPB], gmean[:, b:b + 1].to_broadcast([P, SPB]))
                last = dve.tensor_copy(rstd_t[:, b * SPB:(b + 1) * SPB],
                                       rstd[:, b:b + 1].to_broadcast([P, SPB]))
            setup(last)
            for n0, tiles, wins, mask in ((0, TF, VF, C_OF), (TF * VF, TP, VP, C_OP)):
                for e in range(wins):
                    last = dve.tensor_copy(vm[:, n0 + e:n0 + tiles * wins:wins, :, Q4],
                                           col(mask + e).unsqueeze(2).to_broadcast([P, tiles, 4]))
            last.then_inc(ones_set, 1)
            dve.wait_ge(proj_turned, 1)
            dve.tensor_copy(projT[:], ps[:, 7, 0:2 * P]).then_inc(projT_ready, 1)

            def link(ins, s, n):
                ins.then_inc(dv, 1)
                dve.wait_ge(dv, s * DV + n)

            def normalise(s, p):
                wait(dve, q_p, s - 1)
                wait(dve, xp_ready, s - 1)
                dst = xn[:, p].rearrange("p (w r c) -> p r w c", r=WS, c=WS)
                src = x_all[:, bass.ds(s * SP, SP)].rearrange("p (r w c) -> p r w c", r=WS, c=WS)
                dve.tensor_scalar(dst, src, mean_t[:, bass.ds(s, 1)], rstd_t[:, bass.ds(s, 1)],
                                  ALU.subtract, ALU.mult).then_inc(xn_ready, 1)

            def own_heads(s, pooled):
                ready, free, done, bank, w0 = (
                    (kv_p, out_p, kvc_p, KVP, NW) if pooled else (kv_f, out_f, kvc_f, KVF, 0))
                dve.wait_ge(ready, s + 1)
                wait(dve, free, s)
                own = col(C_HEAD, QG * KC).rearrange("p (j c) -> p j c", c=KC).unsqueeze(1)
                for b in range(2):
                    src = ps[:, bank + b, 0:HALF * VC].rearrange("p (w c) -> p w c", c=VC).unsqueeze(2)
                    dst = kvc[:, w0 + b * HALF:w0 + (b + 1) * HALF]
                    for c0, c1, n0, n1 in ((0, Q4, 0, Q4), (Q4, KC, Q4, VC)):
                        shape = [P, HALF, QG, c1 - c0]
                        last = dve.tensor_tensor(dst[:, :, :, c0:c1], src[:, :, :, n0:n1].to_broadcast(shape),
                                                 own[:, :, :, c0:c1].to_broadcast(shape), ALU.mult)
                last.then_inc(done, 1)

            def divide(s, pooled):
                ready, free, done, bank, w0, wins, mask, step = (
                    (out_p, oT_p, num_p, OUTP, NW, WP, C_WP, 3) if pooled else
                    (out_f, oT_f, num_f, OUTF, 0, WF, C_WF, 0))
                chunks = NW // (wins * QG)
                dve.wait_ge(ready, s + 1)
                src = ps[:, bank:bank + 2, 0:HALF * KC].rearrange("p b (w c) -> p b w c", c=KC)
                r = rm[:, w0:w0 + NW, :]
                nm = num[:, w0:w0 + NW, :]
                link(dve.tensor_scalar(r.rearrange("p (b w) h -> p b w h", b=2), src[:, :, :, Q4:KC],
                                       DEN_EPS, None, ALU.add), s, step + 1)
                link(dve.reciprocal(r, r), s, step + 2)
                link(dve.tensor_tensor(
                    r.rearrange("p (k e j) h -> p k e (j h)", e=wins, j=QG),
                    r.rearrange("p (k e j) h -> p k e (j h)", e=wins, j=QG),
                    col(mask, wins).unsqueeze(1).unsqueeze(3).to_broadcast([P, chunks, wins, QG * 4]),
                    ALU.mult), s, step + 3)
                wait(dve, free, s)
                for b in range(2):
                    h = slice(b * HALF, (b + 1) * HALF)
                    last = dve.tensor_tensor(
                        nm[:, h, :].rearrange("p w (h m) -> p w h m", m=D),
                        src[:, b, :, 0:Q4].rearrange("p w (h m) -> p w h m", m=D),
                        r[:, h, :].unsqueeze(3).to_broadcast([P, HALF, 4, D]), ALU.mult)
                last.then_inc(done, 1)

            def residual(s):
                dve.wait_ge(projected, s + 1)
                xs = x_all[:, bass.ds(s * SP, SP)]
                dve.scalar_tensor_tensor(xs, ps[:, PROJ, 0:SP], shift[:], xs, ALU.add,
                                         ALU.add).then_inc(y_done, 1)

            def step(s, p):
                own_heads(s, False)
                if not isinstance(s, int) or s < NS - 2:
                    normalise(s + 2, p)
                own_heads(s, True)
                divide(s, False)
                if not is_first(s):
                    residual(s - 1)
                divide(s, True)

            normalise(0, 0)
            normalise(1, 1)
            over_strips(dve, step)
            residual(NS - 1)

        @block.tensor
        def _(pe):
            pe.wait_ge(loaded_w, 16 * 5)
            pe.wait_ge(stat_in, 1)
            pe.matmul(ps[:, 6, 0:B], col(C_GROUP, P), dev[:], start=True, stop=True).then_inc(stat_out, 1)
            pe.wait_ge(stat_in, 2)
            pe.matmul(ps[:, 7, 0:B], col(C_GROUP, P), var[:, 0:B], start=True, stop=True).then_inc(stat_out, 1)
            pe.wait_ge(proj_scaled, 1)
            for z in range(2):
                last = pe.transpose(ps[:, 7, z * P:(z + 1) * P], proj_sb[:, z * P:(z + 1) * P], col(C_IDENT, P))
            last.then_inc(proj_turned, 1)
            pe.wait_ge(projT_ready, 1)
            pe.wait_ge(ones_set, 1)

            def conv_kv(s, p):
                pe.wait_ge(xn_ready, s + 1)
                wait(pe, num_p, s - 1)
                for half, bank, done in ((0, K_F, k_f), (1, V_F, v_f)):
                    for t in range(TF):
                        last = pe.matmul(ps[:, bank, t * P:(t + 1) * P], xn[:, p, t * P:(t + 1) * P],
                                         wkv_sb[:, half * P:(half + 1) * P], start=True, stop=True)
                    last.then_inc(done, 1)
                pe.wait_ge(xp_ready, s + 1)
                wait(pe, qm_f, s)
                wait(pe, qm_p, s)
                for half, bank, done in ((0, K_P, k_p), (1, V_P, v_p)):
                    for t in range(TP):
                        last = pe.matmul(ps[:, bank, t * P:(t + 1) * P], xp[:, p, t * P:(t + 1) * P],
                                         wkv_sb[:, half * P:(half + 1) * P], start=True, stop=True)
                    last.then_inc(done, 1)

            def conv_q(s, p):
                pe.wait_ge(km_p, s + 1)
                pe.matmul(ps[:, Q_F, 0:SP], wq_sb[:], xn[:, p], start=True, stop=True).then_inc(q_f, 1)
                pe.wait_ge(vm_p, s + 1)
                pe.matmul(ps[:, Q_P, 0:NW * PXP], wq_sb[:],
                          xp[:, p].rearrange("p (q j) -> p q j", j=Q4)[:, :, 0:WP * PXP],
                          start=True, stop=True).then_inc(q_p, 1)

            def kv_products(s, pooled):
                kmr, vmr, done, bank, t0, n0, tiles, wins = (
                    (km_p, vm_p, kv_p, KVP, TF, TF * VF, TP, VP) if pooled else
                    (km_f, vm_f, kv_f, KVF, 0, 0, TF, VF))
                pe.wait_ge(kmr, s + 1)
                pe.wait_ge(vmr, s + 1)
                if pooled:
                    wait(pe, num_f, s)
                for t in range(tiles):
                    for g in range(G):
                        b, at = divmod((t * G + g) * wins, HALF)
                        if b == 1 and at == 0 and not pooled:
                            wait(pe, y_done, s - 1)
                        for i in range(4):
                            last = pe.matmul(ps[Q4 * i:Q4 * (i + 1), bank + b, at * VC:(at + wins) * VC],
                                             km[:, t0 + t, g, Q4 * i:Q4 * (i + 1)],
                                             vm[:, n0 + t * wins:n0 + (t + 1) * wins, i, :],
                                             start=True, stop=True)
                last.then_inc(done, 1)

            def out_products(s, pooled):
                qmr, kvr, done, bank, t0, w0, tiles, wins = (
                    (qm_p, kvc_p, out_p, OUTP, TF, NW, TP, WP) if pooled else
                    (qm_f, kvc_f, out_f, OUTF, 0, 0, TF, WF))
                pe.wait_ge(qmr, s + 1)
                pe.wait_ge(kvr, s + 1)
                if not pooled:
                    pe.wait_ge(kvc_p, s + 1)
                elif not is_last(s):
                    pe.wait_ge(km_f, s + 2)
                    pe.wait_ge(vm_f, s + 2)
                for t in range(tiles):
                    for g in range(G):
                        b, at = divmod((t * G + g) * wins * QG, HALF)
                        for c in range(4):
                            w = w0 + (t * 4 + c) * wins
                            last = pe.matmul(ps[Q4 * c:Q4 * (c + 1), bank + b, at * KC:(at + wins * QG) * KC],
                                             qm[:, g, (t0 + t) * P + Q4 * c:(t0 + t) * P + Q4 * (c + 1)],
                                             kvc[:, w:w + wins], start=True, stop=True)
                last.then_inc(done, 1)

            def transposes(s):
                pe.wait_ge(oT_f, s + 1)
                pe.wait_ge(oT_p, s + 1)
                if not is_last(s):
                    pe.wait_ge(kvc_f, s + 2)
                else:
                    pe.wait_ge(y_done, s)
                for bank, t0, n, pxs, columns, done in (
                        (TRF, 0, TF, P, C_IDENT, tr_f), (TRP, TF, TP, 4 * WP * PXP, C_PACK, tr_p)):
                    for t in range(n):
                        last = pe.transpose(
                            ps[:, bank, t * pxs:t * pxs + P],
                            oT[:, (t0 + t) * G:(t0 + t + 1) * G, :].rearrange("p i c -> p (i c)"),
                            col(columns, P))
                    last.then_inc(done, 1)

            def project(s):
                pe.wait_ge(o_f, s + 1)
                pe.wait_ge(o_p, s + 1)
                pe.matmul(ps[:, PROJ, 0:SP], projT[:, 0:P], o_sb[:, 0, :], start=True, stop=False)
                pe.matmul(ps[:, PROJ, 0:SP], projT[:, P:2 * P], o_sb[:, 1, :], start=False,
                          stop=True).then_inc(projected, 1)

            def step(s, p):
                kv_products(s, False)
                conv_q(s, p)
                kv_products(s, True)
                if not is_last(s):
                    conv_kv(s + 1, 1 - p)
                if not is_first(s):
                    transposes(s - 1)
                out_products(s, False)
                if not is_first(s):
                    project(s - 1)
                out_products(s, True)

            conv_kv(0, 0)
            over_strips(pe, step)
            transposes(NS - 1)
            project(NS - 1)


def kernel(x, L0_conv_qkv_w, L0_conv_proj_w, L0_conv_bn_gamma, L0_conv_bn_beta, L0_conv_bn_mean,
           L0_conv_bn_var):
    import concourse.bacc as bacc
    from concourse.bass_utils import run_bass_kernel_spmd

    heads = P // D
    w = np.asarray(L0_conv_qkv_w).reshape(heads, 3, D, P).transpose(1, 3, 0, 2).reshape(3, P, P)
    arrays = {
        "x": np.ascontiguousarray(x),
        "wq": np.ascontiguousarray(w[0]),
        "wkv": np.ascontiguousarray(np.concatenate([w[1], w[2]], axis=1)),
        "proj": np.ascontiguousarray(L0_conv_proj_w),
        "bn": np.stack([np.asarray(a) for a in (L0_conv_bn_gamma, L0_conv_bn_beta, L0_conv_bn_mean,
                                                L0_conv_bn_var)], axis=1),
        "consts": constants(),
    }
    nc = bacc.Bacc("TRN2", target_bir_lowering=False, num_devices=1)
    aps = {n: nc.dram_tensor(n, a.shape, mybir.dt.from_np(a.dtype), kind="ExternalInput").ap()
           for n, a in arrays.items()}
    out = nc.dram_tensor("out", arrays["x"].shape, F32, kind="ExternalOutput").ap()
    build(nc, **aps, out=out)
    r = run_bass_kernel_spmd(nc, [arrays], core_ids=[0])
    return r.results[0]["out"]
```

```python
from contextlib import ExitStack

import numpy as np

import concourse.bass as bass
from concourse import mybir

F32 = mybir.dt.float32
ALU = mybir.AluOpType
ACT = mybir.ActivationFunctionType

P = 128
Q4 = 32
WS = 4
D = 8
GROUPS = 32
GN_EPS, BN_EPS, DEN_EPS = 1e-5, 1e-5, 1e-15

PX = WS * WS
PXP = 9
NP = WS - 1
WF = Q4 // PX
WP = Q4 // PXP
VC = Q4 + 1
KC = Q4 + 4
G = 2
QG = 4 // G

C_IDENT, C_GROUP = 0, P
C_HEAD = 2 * P
C_HALF = C_HEAD + QG * KC
C_HALFP = C_HALF + G
C_VF = C_HALFP + G
C_VP = C_VF + 4 * WF
C_OP = C_VP + QG * WP
C_WF = C_OP + QG * WP
C_WP = C_WF + WF
C_PACK = C_WP + WP
N_CONST = C_PACK + P


def constants():
    c = np.zeros((P, N_CONST), np.float32)
    p = np.arange(P)
    c[:, C_IDENT:C_IDENT + P] = np.eye(P)
    per = P // GROUPS
    c[:, C_GROUP:C_GROUP + P] = (p[:, None] // per == p[None] // per) / per
    quad, head = p // Q4, p % Q4 // D
    for j in range(QG):
        at = C_HEAD + j * KC
        mine = quad[:, None] % QG == j
        c[:, at:at + Q4] = mine & (head[:, None] == np.arange(Q4)[None] // D)
        c[:, at + Q4:at + KC] = mine & (head[:, None] == np.arange(4)[None])
    half = quad[:, None] // QG == np.arange(G)[None]
    c[:, C_HALF:C_HALF + G] = half
    c[:, C_HALFP:C_HALFP + G] = half / 25.0
    win_f, win_p = p % Q4 // PX, p % Q4 // PXP
    side = np.array([1, 2, 1])
    times = (side[:, None] * side[None]).ravel()[p % Q4 % PXP][:, None]
    own_f = (quad * WF + win_f)[:, None] == np.arange(4 * WF)[None]
    own_p = ((quad % QG * WP + win_p)[:, None] == np.arange(QG * WP)[None]) & (win_p < WP)[:, None]
    c[:, C_VF:C_VF + 4 * WF] = own_f
    c[:, C_VP:C_VP + QG * WP] = own_p * times / 25.0
    c[:, C_OP:C_OP + QG * WP] = own_p * times
    c[:, C_WF:C_WF + WF] = win_f[:, None] == np.arange(WF)[None]
    c[:, C_WP:C_WP + WP] = win_p[:, None] == np.arange(WP)[None]
    pads = p % Q4 >= WP * PXP
    c[np.concatenate([p[~pads], p[pads]]), C_PACK + p] = 1
    return c


def build(nc, x, wq, wkv, proj, bn, consts, out):
    B, C, H, W = x.shape
    assert C == P
    HW = H * W
    SPB = H // WS
    NS = B * SPB
    SP = WS * W
    NW = W // WS
    TF = SP // P
    TP = NW // (4 * WP)
    assert TF * P == SP and TP * 4 * WP == NW
    HALF = NW // 2
    assert HALF * KC <= 512
    VF, VP = 4 * WF, QG * WP
    TV = TF + TP
    FOURS = SPB // 4
    GROUPING = 3 + 2 * FOURS
    assert FOURS * 4 == SPB and GROUPING + 4 < SPB and (SPB + 3 - GROUPING) % 2 == 0

    x_v = x.rearrange("b c h w -> c b (h w)")
    out_v = out.rearrange("b c h w -> c b (h w)")

    with ExitStack() as ctx:
        def sb(name, shape):
            return ctx.enter_context(nc.sbuf_tensor(name, [P, *shape], F32))

        def sem(name):
            return ctx.enter_context(nc.semaphore(name))

        x_all = sb("x_all", [NS * SP])
        cst = sb("cst", [N_CONST])
        wq_sb = sb("wq_sb", [P])
        wkv_sb = sb("wkv_sb", [2 * P])
        projT = sb("projT", [2 * P])
        bn_sb = sb("bn_sb", [4])
        bn_inv = sb("bn_inv", [1])
        bn_off = sb("bn_off", [1])
        shift = sb("shift", [1])
        stats = sb("stats", [SPB, 6])
        mv = sb("mv", [2])
        total = sb("total", [1])
        dev = sb("dev", [1])
        var_g = sb("var_g", [1])
        var = sb("var", [1])
        std = sb("std", [1])
        root = sb("root", [1])
        fix = sb("fix", [1])
        mean_t = sb("mean_t", [NS])
        rstd_t = sb("rstd_t", [NS])
        xn = sb("xn", [2, SP])
        hs = sb("hs", [NW, WS, NP])
        ht = sb("ht", [NW, WS])
        vt = sb("vt", [NW, NP])
        xp = sb("xp", [2, TP * P])
        k_full = sb("k_full", [TF, P])
        km = sb("km", [TP, G, P])
        vm = sb("vm", [TF * VF + TP * VP, 4, VC])
        qm = sb("qm", [G, TV * P])
        kvc = sb("kvc", [2 * NW, QG, KC])
        rm = sb("rm", [2 * NW, 4])
        num = sb("num", [NW, Q4])
        oT = sb("oT", [TV * G, QG * Q4])
        o_sb = sb("o_sb", [SP + NW * PXP])
        proj_sb = o_sb[:, 0:2 * P]

        ps = ctx.enter_context(nc.psum_tensor("ps", [P, 8, 512], F32))
        KVF = 0
        TRF, TRP = 0, 1
        Y_F, Y_P = 0, 1
        K_F, V_F = 2, 3
        OUTP = 2
        KVP = 4
        GROUP = HALF * KC
        OUTF = 4
        K_P, V_P = 6, 7
        Q_F, Q_P = 6, 7

        loaded_w = sem("loaded_w")
        loaded_first = [sem(f"loaded_first{i}") for i in range(FOURS)]
        loaded_batch = [sem(f"loaded_batch{b}") for b in range(1, B)]
        dv_setup = sem("dv_setup")
        dv_group = sem("dv_group")
        dv = sem("dv")
        pl = sem("pl")
        gathered = sem("gathered")
        pads_zero = sem("pads_zero")
        ones_set = sem("ones_set")
        stat_in = sem("stat_in")
        stat_out = sem("stat_out")
        var_ready = sem("var_ready")
        std_ready = sem("std_ready")
        proj_scaled = sem("proj_scaled")
        proj_turned = sem("proj_turned")
        projT_ready = sem("projT_ready")
        xn_ready, xp_ready = sem("xn_ready"), sem("xp_ready")
        k_f, v_f, k_p, v_p = sem("k_f"), sem("v_f"), sem("k_p"), sem("v_p")
        q_f, q_p = sem("q_f"), sem("q_p")
        km_f, km_p = sem("km_f"), sem("km_p")
        vm_f, vm_p = sem("vm_f"), sem("vm_p")
        qm_f, qm_p = sem("qm_f"), sem("qm_p")
        kv_f, kv_p = sem("kv_f"), sem("kv_p")
        kvc_f, kvc_p = sem("kvc_f"), sem("kvc_p")
        out_f, out_p = sem("out_f"), sem("out_p")
        num_f, num_p = sem("num_f"), sem("num_p")
        two_ready = sem("two_ready")
        oT_f, oT_p = sem("oT_f"), sem("oT_p")
        tr_f, tr_p = sem("tr_f"), sem("tr_p")
        o_f, o_p = sem("o_f"), sem("o_p")
        y_f, y_p = sem("y_f"), sem("y_p")
        added_f = sem("added_f")
        y_done = sem("y_done")
        stored = sem("stored")

        def col(i, n=1):
            return cst[:, i:i + n]

        def wait(eng, semaphore, value):
            if not (isinstance(value, int) and value <= 0):
                eng.wait_ge(semaphore, value)

        def over_strips(eng, step):
            for s in (0, 1, 2):
                step(s, s % 2)
            with eng.Fori(0, B - 1) as b:
                with eng.Fori(0, FOURS) as i:
                    s = b * SPB + i * 2 + 3
                    step(s, 1, gather=(b + 1, i, 0))
                    step(s + 1, 0, gather=(b + 1, i, 2))
                for phase in range(4):
                    step(b * SPB + (GROUPING + phase), (GROUPING + phase) % 2, group=(b + 1, phase))
                with eng.Fori(GROUPING + 4, SPB + 3, 2) as t:
                    step(b * SPB + t, 1)
                    step(b * SPB + t + 1, 0)
            with eng.Fori((B - 1) * SPB + 3, NS - 3, 2) as s:
                step(s, 1)
                step(s + 1, 0)
            for s in (NS - 3, NS - 2, NS - 1):
                step(s, s % 2)

        def is_last(s):
            return isinstance(s, int) and s == NS - 1

        def is_first(s):
            return isinstance(s, int) and s == 0

        block = ctx.enter_context(nc.Block())

        @block.sync
        def _(sp):
            for i in range(FOURS):
                sp.dma_start(x_all[:, 4 * i * SP:4 * (i + 1) * SP],
                             x_v[:, 0, 4 * i * SP:4 * (i + 1) * SP]).then_inc(loaded_first[i], 16)
            for dst, src in ((cst[:], consts), (wkv_sb[:], wkv), (wq_sb[:], wq), (bn_sb[:], bn), (proj_sb, proj)):
                sp.dma_start(dst, src).then_inc(loaded_w, 16)
            for b in range(1, B):
                sp.dma_start(x_all[:, b * HW:(b + 1) * HW], x_v[:, b]).then_inc(loaded_batch[b - 1], 16)
            for b in range(B):
                with sp.Fori(0, SPB) as t:
                    sp.wait_ge(y_done, t + (b * SPB + 1))
                    sp.dma_start(out_v[:, b, bass.ds(t * SP, SP)],
                                 x_all[:, bass.ds(t * SP + b * HW, SP)]).then_inc(stored, 16)
            sp.wait_ge(stored, 16 * NS)

        @block.gpsimd
        def _(pool):
            PL = 6
            pool.memset(xp[:], 0.0).then_inc(pads_zero, 1)
            pool.memset(qm[:], 0.0).then_inc(pads_zero, 1)

            def add(o, a, b):
                return pool.tensor_tensor(o, a, b, ALU.add)

            def pooling(s, p):
                xv = xn[:, p].rearrange("p (w r c) -> p w r c", r=WS, c=WS)
                xo = xp[:, p].rearrange("p (q j) -> p q j", j=Q4)[:, :, 0:WP * PXP].rearrange(
                    "p q (w r c) -> p q w r c", w=WP, c=NP)
                h3 = hs[:].rearrange("p (q w) r c -> p q w r c", w=WP)
                v3 = vt[:].rearrange("p (q w) c -> p q w c", w=WP)

                def link(ins, n):
                    ins.then_inc(pl, 1)
                    pool.wait_ge(pl, s * PL + n)

                pool.wait_ge(xn_ready, s + 1)
                link(add(ht[:], xv[:, :, :, 1], xv[:, :, :, 2]), 1)
                link(add(hs[:, :, :, 0], ht[:], xv[:, :, :, 0]), 2)
                add(hs[:, :, :, 2], ht[:], xv[:, :, :, 3])
                link(add(hs[:, :, :, 1], hs[:, :, :, 0], xv[:, :, :, 3]), 3)
                link(add(vt[:], hs[:, :, 1, :], hs[:, :, 2, :]), 4)
                wait(pool, q_p, s - 1)
                link(add(xo[:, :, :, 0, :], v3, h3[:, :, :, 0, :]), 5)
                add(xo[:, :, :, 2, :], v3, h3[:, :, :, 3, :]).then_inc(pl, 1)
                add(xo[:, :, :, 1, :], xo[:, :, :, 0, :], h3[:, :, :, 3, :]).then_inc(xp_ready, 1)

            pool.wait_ge(pads_zero, 2)

            def own_window(s):
                pool.wait_ge(num_f, s + 1)
                wait(pool, tr_f, s)
                nf = num[:].rearrange("p (k e j) c -> p k e (j c)", e=WF, j=QG)
                add(oT[:, 0:TF * G, :], nf[:, :, 0], nf[:, :, 1]).then_inc(oT_f, 1)

            def own_window_pooled(s):
                pool.wait_ge(num_p, s + 1)
                np_ = num[:].rearrange("p (k e j) c -> p k e (j c)", e=WP, j=QG)
                add(np_[:, :, 0], np_[:, :, 0], np_[:, :, 1]).then_inc(two_ready, 1)
                wait(pool, tr_p, s)
                pool.wait_ge(two_ready, s + 1)
                add(oT[:, TF * G:TV * G, :], np_[:, :, 0], np_[:, :, 2]).then_inc(oT_p, 1)

            def step(s, p, gather=None, group=None):
                if not isinstance(s, int) or s < NS - 2:
                    pooling(s + 2, p)
                own_window(s)
                own_window_pooled(s)

            pooling(0, 0)
            pooling(1, 1)
            over_strips(pool, step)

        @block.scalar
        def _(act):
            def copied_k(s):
                act.wait_ge(k_f, s + 1)
                wait(act, kv_f, s)
                act.activation(k_full[:].rearrange("p t c -> p (t c)"), ps[:, K_F, 0:TF * P],
                               ACT.Relu).then_inc(km_f, 1)

            def masked_k(s):
                act.wait_ge(k_p, s + 1)
                wait(act, kv_p, s)
                for g in range(G):
                    last = act.activation(km[:, :, g, :],
                                          ps[:, K_P, 0:TP * P].rearrange("p (t c) -> p t c", c=P),
                                          ACT.Relu, scale=col(C_HALFP + g))
                last.then_inc(km_p, 1)

            def masked_v(s, pooled):
                ready, free, done, bank, n0, tiles, wins, mask = (
                    (v_p, kv_p, vm_p, V_P, TF * VF, TP, VP, C_VP) if pooled else
                    (v_f, kv_f, vm_f, V_F, 0, TF, VF, C_VF))
                act.wait_ge(ready, s + 1)
                wait(act, free, s)
                for j in range(wins):
                    last = act.activation(
                        vm[:, n0 + j:n0 + tiles * wins:wins, :, 0:Q4],
                        ps[:, bank, 0:tiles * P].rearrange("p (t i c) -> p t i c", i=4, c=Q4),
                        ACT.Copy, scale=col(mask + j))
                last.then_inc(done, 1)

            def masked_q(s):
                for ready, free, done, bank, at, used, n, mask in (
                        (q_f, out_f, qm_f, Q_F, 0, Q4, TF * 4, C_HALF),
                        (q_p, out_p, qm_p, Q_P, TF * P, WP * PXP, TP * 4, C_HALFP)):
                    act.wait_ge(ready, s + 1)
                    wait(act, free, s)
                    for i in range(G):
                        last = act.activation(
                            qm[:, i, at:at + n * Q4].rearrange("p (q j) -> p q j", j=Q4)[:, :, 0:used],
                            ps[:, bank, 0:n * used].rearrange("p (q j) -> p q j", j=used),
                            ACT.Relu, scale=col(mask + i))
                    last.then_inc(done, 1)

            def to_image(s):
                act.wait_ge(tr_f, s + 1)
                wait(act, y_f, s)
                act.activation(o_sb[:, 0:SP].rearrange("p (r w c) -> p w r c", r=WS, c=WS),
                               ps[:, TRF, 0:SP].rearrange("p (w r c) -> p w r c", r=WS, c=WS),
                               ACT.Copy).then_inc(o_f, 1)

            def square_root(n):
                act.wait_ge(var_ready, n + 1)
                act.activation(std[:], var[:], ACT.Sqrt).then_inc(std_ready, 1)

            square_root(0)
            square_root(1)
            act.wait_ge(loaded_w, 16 * 5)
            act.wait_ge(pads_zero, 2)

            def step(s, p, gather=None, group=None):
                masked_q(s)
                if not is_last(s):
                    copied_k(s + 1)
                if not is_first(s):
                    to_image(s - 1)
                if not is_last(s):
                    masked_v(s + 1, False)
                    masked_k(s + 1)
                    masked_v(s + 1, True)
                if group and group[1] == 2:
                    square_root(group[0] + 1)

            copied_k(0)
            masked_v(0, False)
            masked_k(0)
            masked_v(0, True)
            over_strips(act, step)
            to_image(NS - 1)

        @block.vector
        def _(dve):
            count = [0]
            DV = 6

            def setup(ins):
                count[0] += 1
                ins.then_inc(dv_setup, 1)
                dve.wait_ge(dv_setup, count[0])

            def gather_strip(b, at):
                return dve.bn_stats(stats[:, bass.ds(at, 1), :].rearrange("p o c -> p (o c)"),
                                    x_all[:, bass.ds(b * HW + at * SP, SP)])

            GS = 8

            def channel_stats():
                dve.bn_aggr(mv[:], stats[:].rearrange("p n c -> p (n c)")).then_inc(stat_in, 1)

            def group_total(b, half):
                dve.wait_ge(stat_out, b * 2 + (half + 1))
                dve.tensor_copy(total[:], ps[:, KVP, GROUP:GROUP + 1]).then_inc(dv_group, 1)

            def group_mean(b):
                dve.wait_ge(dv_group, b * GS + 1)
                dve.tensor_copy(mean_t[:, bass.ds(b * SPB, SPB)], total[:].to_broadcast([P, SPB])).then_inc(dv_group, 1)
                dve.tensor_tensor(dev[:], mv[:, 0:1], total[:], ALU.subtract).then_inc(dv_group, 1)
                dve.wait_ge(dv_group, b * GS + 3)
                dve.tensor_scalar(var_g[:], dev[:], dev[:], mv[:, 1:2], ALU.mult, ALU.add).then_inc(stat_in, 1)

            def group_var(b):
                dve.wait_ge(dv_group, b * GS + 4)
                dve.tensor_scalar(var[:], total[:], GN_EPS, None, ALU.add).then_inc(var_ready, 1)

            def group_rstd(b, square_roots):
                dve.wait_ge(std_ready, square_roots)
                dve.reciprocal(root[:], std[:]).then_inc(dv_group, 1)
                dve.wait_ge(dv_group, b * GS + 5)
                dve.tensor_scalar(fix[:], root[:], root[:], var[:], ALU.mult, ALU.mult).then_inc(dv_group, 1)
                dve.wait_ge(dv_group, b * GS + 6)
                dve.tensor_scalar(fix[:], fix[:], -0.5, 1.5, ALU.mult, ALU.add).then_inc(dv_group, 1)
                dve.wait_ge(dv_group, b * GS + 7)
                dve.tensor_scalar(rstd_t[:, bass.ds(b * SPB, SPB)], fix[:].to_broadcast([P, SPB]),
                                  root[:], None, ALU.mult).then_inc(dv_group, 1)
                dve.wait_ge(dv_group, b * GS + 8)

            for i in range(FOURS):
                dve.wait_ge(loaded_first[i], 16)
                for at in range(4 * i, 4 * i + 4):
                    last = gather_strip(0, at)
                last.then_inc(gathered, 1)
            dve.wait_ge(gathered, FOURS)
            channel_stats()
            group_total(0, 0)
            group_mean(0)
            group_total(0, 1)
            group_var(0)
            group_rstd(0, 1)

            def link(ins, s, n):
                ins.then_inc(dv, 1)
                dve.wait_ge(dv, s * DV + n)

            def normalise(s, p):
                wait(dve, q_p, s - 1)
                wait(dve, xp_ready, s - 1)
                dst = xn[:, p].rearrange("p (w r c) -> p r w c", r=WS, c=WS)
                src = x_all[:, bass.ds(s * SP, SP)].rearrange("p (r w c) -> p r w c", r=WS, c=WS)
                dve.tensor_scalar(dst, src, mean_t[:, bass.ds(s, 1)], rstd_t[:, bass.ds(s, 1)],
                                  ALU.subtract, ALU.mult).then_inc(xn_ready, 1)

            def own_heads(s, pooled):
                ready, free, done, bank, w0 = (
                    (kv_p, out_p, kvc_p, KVP, NW) if pooled else (kv_f, out_f, kvc_f, KVF, 0))
                dve.wait_ge(ready, s + 1)
                wait(dve, free, s)
                own = col(C_HEAD, QG * KC).rearrange("p (j c) -> p j c", c=KC).unsqueeze(1)
                for b in range(2):
                    src = ps[:, bank + b, 0:HALF * VC].rearrange("p (w c) -> p w c", c=VC).unsqueeze(2)
                    dst = kvc[:, w0 + b * HALF:w0 + (b + 1) * HALF]
                    for c0, c1, n0, n1 in ((0, Q4, 0, Q4), (Q4, KC, Q4, VC)):
                        shape = [P, HALF, QG, c1 - c0]
                        last = dve.tensor_tensor(dst[:, :, :, c0:c1], src[:, :, :, n0:n1].to_broadcast(shape),
                                                 own[:, :, :, c0:c1].to_broadcast(shape), ALU.mult)
                last.then_inc(done, 1)

            def pooled_out(s):
                dve.wait_ge(tr_p, s + 1)
                wait(dve, y_p, s)
                dve.tensor_copy(o_sb[:, SP:], ps[:, TRP, 0:NW * PXP]).then_inc(o_p, 1)

            def residual(s):
                dve.wait_ge(y_f, s + 1)
                xs = x_all[:, bass.ds(s * SP, SP)]
                dve.scalar_tensor_tensor(xs, ps[:, Y_F, 0:SP], shift[:], xs, ALU.add,
                                         ALU.add).then_inc(added_f, 1)
                dve.wait_ge(y_p, s + 1)
                dve.wait_ge(added_f, s + 1)
                src = ps[:, Y_P, 0:NW * PXP].rearrange("p (w r c) -> p w r c", r=NP, c=NP)
                dst = xs.rearrange("p (r w c) -> p w r c", r=WS, c=WS)
                ends, ends_p, mid, mid_p = slice(0, WS, WS - 1), slice(0, NP, NP - 1), slice(1, 3), slice(1, 2)
                for rows, rows_p in ((ends, ends_p), (mid, mid_p)):
                    for cols, cols_p in ((ends, ends_p), (mid, mid_p)):
                        part = dst[:, :, rows, cols]
                        last = dve.tensor_tensor(part, src[:, :, rows_p, cols_p].to_broadcast([P, NW, 2, 2]),
                                                 part, ALU.add)
                last.then_inc(y_done, 1)

            def divide(s, pooled):
                ready, done, bank, w0, wins, mask, step = (
                    (out_p, num_p, OUTP, NW, WP, C_WP, 3) if pooled else (out_f, num_f, OUTF, 0, WF, C_WF, 0))
                chunks = NW // (wins * QG)
                dve.wait_ge(ready, s + 1)
                src = ps[:, bank:bank + 2, 0:HALF * KC].rearrange("p b (w c) -> p b w c", c=KC)
                r = rm[:, w0:w0 + NW, :]
                link(dve.tensor_scalar(r.rearrange("p (b w) h -> p b w h", b=2), src[:, :, :, Q4:KC],
                                       DEN_EPS, None, ALU.add), s, step + 1)
                link(dve.reciprocal(r, r), s, step + 2)
                link(dve.tensor_tensor(
                    r.rearrange("p (k e j) h -> p k e (j h)", e=wins, j=QG),
                    r.rearrange("p (k e j) h -> p k e (j h)", e=wins, j=QG),
                    col(mask, wins).unsqueeze(1).unsqueeze(3).to_broadcast([P, chunks, wins, QG * 4]),
                    ALU.mult), s, step + 3)
                if pooled:
                    dve.wait_ge(oT_f, s + 1)
                else:
                    wait(dve, oT_p, s)
                for b in range(2):
                    h = slice(b * HALF, (b + 1) * HALF)
                    last = dve.tensor_tensor(
                        num[:, h, :].rearrange("p w (h m) -> p w h m", m=D),
                        src[:, b, :, 0:Q4].rearrange("p w (h m) -> p w h m", m=D),
                        r[:, h, :].unsqueeze(3).to_broadcast([P, HALF, 4, D]), ALU.mult)
                last.then_inc(done, 1)

            def step(s, p, gather=None, group=None):
                b, phase = group or (None, None)
                own_heads(s, False)
                if phase == 0:
                    dve.wait_ge(gathered, b * FOURS + FOURS)
                if phase in (1, 2):
                    group_total(b, phase - 1)
                own_heads(s, True)
                if not is_first(s):
                    pooled_out(s - 1)
                if not isinstance(s, int) or s < NS - 2:
                    normalise(s + 2, p)
                if gather:
                    gb, i, first = gather
                    gather_strip(gb, i * 4 + first)
                    last = gather_strip(gb, i * 4 + (first + 1))
                    if first:
                        last.then_inc(gathered, 1)
                if phase == 0:
                    channel_stats()
                elif phase == 1:
                    group_mean(b)
                elif phase == 2:
                    group_var(b)
                elif phase == 3:
                    group_rstd(b, b + 2)
                if isinstance(s, int) and s == 2:
                    for loaded in loaded_batch:
                        dve.wait_ge(loaded, 16)
                if not is_first(s):
                    residual(s - 1)
                divide(s, False)
                divide(s, True)

            normalise(0, 0)
            normalise(1, 1)
            dve.wait_ge(loaded_w, 16 * 5)
            dve.tensor_scalar(var[:], bn_sb[:, 3:4], BN_EPS, None, ALU.add).then_inc(var_ready, 1)
            dve.wait_ge(std_ready, 2)
            setup(dve.reciprocal(root[:], std[:]))
            setup(dve.tensor_scalar(fix[:], root[:], root[:], var[:], ALU.mult, ALU.mult))
            setup(dve.tensor_scalar(fix[:], fix[:], -0.5, 1.5, ALU.mult, ALU.add))
            setup(dve.tensor_scalar(bn_inv[:], root[:], fix[:], bn_sb[:, 0:1], ALU.mult, ALU.mult))
            setup(dve.tensor_tensor(bn_off[:], bn_sb[:, 2:3], bn_inv[:], ALU.mult))
            setup(dve.tensor_tensor(shift[:], bn_sb[:, 1:2], bn_off[:], ALU.subtract))
            dve.tensor_scalar(proj_sb, proj_sb, bn_inv[:], None, ALU.mult).then_inc(proj_scaled, 1)
            for n0, tiles, wins, mask in ((0, TF, VF, C_VF), (TF * VF, TP, VP, C_OP)):
                for e in range(wins):
                    last = dve.tensor_copy(vm[:, n0 + e:n0 + tiles * wins:wins, :, Q4],
                                           col(mask + e).unsqueeze(2).to_broadcast([P, tiles, 4]))
            last.then_inc(ones_set, 1)
            dve.wait_ge(proj_turned, 1)
            dve.tensor_copy(projT[:], ps[:, TRF, 0:2 * P]).then_inc(projT_ready, 1)
            over_strips(dve, step)
            pooled_out(NS - 1)
            residual(NS - 1)

        @block.tensor
        def _(pe):
            def group_average(b, half):
                pe.wait_ge(stat_in, b * 2 + (half + 1))
                pe.matmul(ps[:, KVP, GROUP:GROUP + 1], col(C_GROUP, P), (mv[:, 0:1], var_g[:])[half],
                          start=True, stop=True).then_inc(stat_out, 1)

            pe.wait_ge(loaded_w, 16 * 5)
            group_average(0, 0)
            group_average(0, 1)

            def conv_kv(s, p):
                pe.wait_ge(xn_ready, s + 1)
                wait(pe, num_p, s - 1)
                for half, bank, done in ((0, K_F, k_f), (1, V_F, v_f)):
                    for t in range(TF):
                        last = pe.matmul(ps[:, bank, t * P:(t + 1) * P], xn[:, p, t * P:(t + 1) * P],
                                         wkv_sb[:, half * P:(half + 1) * P], start=True, stop=True)
                    last.then_inc(done, 1)

            def conv_kv_pooled(s, p):
                pe.wait_ge(xp_ready, s + 1)
                wait(pe, qm_f, s)
                wait(pe, qm_p, s)
                for half, bank, done in ((0, K_P, k_p), (1, V_P, v_p)):
                    for t in range(TP):
                        last = pe.matmul(ps[:, bank, t * P:(t + 1) * P], xp[:, p, t * P:(t + 1) * P],
                                         wkv_sb[:, half * P:(half + 1) * P], start=True, stop=True)
                    last.then_inc(done, 1)

            def conv_q(s, p):
                pe.wait_ge(km_p, s + 1)
                pe.matmul(ps[:, Q_F, 0:SP], wq_sb[:], xn[:, p], start=True, stop=True).then_inc(q_f, 1)
                pe.wait_ge(vm_p, s + 1)
                pe.matmul(ps[:, Q_P, 0:NW * PXP], wq_sb[:],
                          xp[:, p].rearrange("p (q j) -> p q j", j=Q4)[:, :, 0:WP * PXP],
                          start=True, stop=True).then_inc(q_p, 1)

            def kv_products(s):
                pe.wait_ge(km_f, s + 1)
                pe.wait_ge(vm_f, s + 1)
                wait(pe, added_f, s - 1)
                edges = sorted({VF * t for t in range(TF + 1)} | {HALF})
                for w0, w1 in zip(edges, edges[1:]):
                    bank, at = divmod(w0, HALF)
                    if w0 == HALF:
                        wait(pe, y_done, s - 1)
                    for i in range(4):
                        last = pe.matmul(ps[Q4 * i:Q4 * (i + 1), KVF + bank, at * VC:(at + w1 - w0) * VC],
                                         k_full[:, w0 // VF, Q4 * i:Q4 * (i + 1)], vm[:, w0:w1, i, :],
                                         start=True, stop=True)
                last.then_inc(kv_f, 1)

            def kv_products_pooled(s):
                pe.wait_ge(km_p, s + 1)
                pe.wait_ge(vm_p, s + 1)
                wait(pe, num_f, s)
                for t in range(TP):
                    for g in range(G):
                        bank, at = divmod((t * G + g) * VP, HALF)
                        for i in range(4):
                            n0 = TF * VF + t * VP
                            last = pe.matmul(ps[Q4 * i:Q4 * (i + 1), KVP + bank, at * VC:(at + VP) * VC],
                                             km[:, t, g, Q4 * i:Q4 * (i + 1)], vm[:, n0:n0 + VP, i, :],
                                             start=True, stop=True)
                last.then_inc(kv_p, 1)

            def out_products(s, pooled):
                qmr, kvr, done, bank, t0, w0, tiles, wins = (
                    (qm_p, kvc_p, out_p, OUTP, TF, NW, TP, WP) if pooled else
                    (qm_f, kvc_f, out_f, OUTF, 0, 0, TF, WF))
                pe.wait_ge(qmr, s + 1)
                pe.wait_ge(kvr, s + 1)
                if not pooled:
                    pe.wait_ge(kvc_p, s + 1)
                elif not is_last(s):
                    pe.wait_ge(km_f, s + 2)
                for t in range(tiles):
                    for g in range(G):
                        b, at = divmod((t * G + g) * wins * QG, HALF)
                        if b == 1 and at == 0 and pooled and not is_last(s):
                            pe.wait_ge(vm_f, s + 2)
                        for c in range(4):
                            w = w0 + (t * 4 + c) * wins
                            last = pe.matmul(ps[Q4 * c:Q4 * (c + 1), bank + b, at * KC:(at + wins * QG) * KC],
                                             qm[:, g, (t0 + t) * P + Q4 * c:(t0 + t) * P + Q4 * (c + 1)],
                                             kvc[:, w:w + wins], start=True, stop=True)
                last.then_inc(done, 1)

            def transposes(s):
                pe.wait_ge(oT_f, s + 1)
                pe.wait_ge(oT_p, s + 1)
                if not is_last(s):
                    pe.wait_ge(kvc_f, s + 2)
                else:
                    pe.wait_ge(added_f, s)
                    pe.wait_ge(y_done, s)
                for bank, t0, n, pxs, columns, done in (
                        (TRF, 0, TF, P, C_IDENT, tr_f), (TRP, TF, TP, 4 * WP * PXP, C_PACK, tr_p)):
                    for t in range(n):
                        last = pe.transpose(
                            ps[:, bank, t * pxs:t * pxs + P],
                            oT[:, (t0 + t) * G:(t0 + t + 1) * G, :].rearrange("p i c -> p (i c)"),
                            col(columns, P))
                    last.then_inc(done, 1)

            def project(s):
                pe.wait_ge(o_f, s + 1)
                pe.matmul(ps[:, Y_F, 0:SP], projT[:, 0:P], o_sb[:, 0:SP], start=True, stop=True).then_inc(y_f, 1)
                pe.wait_ge(o_p, s + 1)
                pe.matmul(ps[:, Y_P, 0:NW * PXP], projT[:, P:2 * P], o_sb[:, SP:],
                          start=True, stop=True).then_inc(y_p, 1)

            def step(s, p, gather=None, group=None):
                kv_products(s)
                kv_products_pooled(s)
                if group and group[1] in (1, 2):
                    group_average(group[0], group[1] - 1)
                conv_q(s, p)
                if not is_last(s):
                    conv_kv(s + 1, 1 - p)
                if not is_first(s):
                    transposes(s - 1)
                if not is_last(s):
                    conv_kv_pooled(s + 1, 1 - p)
                if not is_first(s):
                    project(s - 1)
                out_products(s, False)
                out_products(s, True)

            conv_kv(0, 0)
            conv_kv_pooled(0, 0)
            pe.wait_ge(proj_scaled, 1)
            for z in range(2):
                last = pe.transpose(ps[:, TRF, z * P:(z + 1) * P], proj_sb[:, z * P:(z + 1) * P], col(C_IDENT, P))
            last.then_inc(proj_turned, 1)
            pe.wait_ge(projT_ready, 1)
            pe.wait_ge(ones_set, 1)
            over_strips(pe, step)
            transposes(NS - 1)
            project(NS - 1)


def kernel(x, L0_conv_qkv_w, L0_conv_proj_w, L0_conv_bn_gamma, L0_conv_bn_beta, L0_conv_bn_mean,
           L0_conv_bn_var):
    import concourse.bacc as bacc
    from concourse.bass_utils import run_bass_kernel_spmd

    heads = P // D
    w = np.asarray(L0_conv_qkv_w).reshape(heads, 3, D, P).transpose(1, 3, 0, 2).reshape(3, P, P)
    arrays = {
        "x": np.ascontiguousarray(x),
        "wq": np.ascontiguousarray(w[0]),
        "wkv": np.ascontiguousarray(np.concatenate([w[1], w[2]], axis=1)),
        "proj": np.ascontiguousarray(L0_conv_proj_w),
        "bn": np.stack([np.asarray(a) for a in (L0_conv_bn_gamma, L0_conv_bn_beta, L0_conv_bn_mean,
                                                L0_conv_bn_var)], axis=1),
        "consts": constants(),
    }
    nc = bacc.Bacc("TRN2", target_bir_lowering=False, num_devices=1)
    aps = {n: nc.dram_tensor(n, a.shape, mybir.dt.from_np(a.dtype), kind="ExternalInput").ap()
           for n, a in arrays.items()}
    out = nc.dram_tensor("out", arrays["x"].shape, F32, kind="ExternalOutput").ap()
    build(nc, **aps, out=out)
    r = run_bass_kernel_spmd(nc, [arrays], core_ids=[0])
    return r.results[0]["out"]
```
